# Optimizing a Trainium2 kernel written in Bass

```python
import numpy as np
import jax
import jax.numpy as jnp

def _softmax(x, axis=-1):
    return jax.nn.softmax(x, axis=axis)

def _gelu(x):
    return jax.nn.gelu(x, approximate=True)

def _silu(x):
    return jax.nn.silu(x)

def _sigmoid(x):
    return jax.nn.sigmoid(x)

def _layernorm(x, axis=-1, eps=1e-05):
    m = jnp.mean(x, axis=axis, keepdims=True)
    v = jnp.var(x, axis=axis, keepdims=True)
    return (x - m) / jnp.sqrt(v + eps)

def _scatter_add(tgt, idx, src, axis=0):
    return tgt.at[idx].add(src)

def _segment_sum(src, seg, n):
    return jax.ops.segment_sum(src, seg, n)
kernel_name = 'mk_prb_d1_jaxref_r4_b561d4'

def setup_inputs(seed: int=0):
    np.random.seed(seed)
    _w = jnp.asarray

    def _L0_attn_setup():
        import jax, jax.numpy as jnp
        import numpy as np
        D_MODEL = 512
        NUM_HEADS = 16
        DK = D_MODEL // NUM_HEADS
        key = jax.random.key(seed)
        kx, kq, kk, kv, ko = jax.random.split(key, 5)
        s = 1.0 / np.sqrt(D_MODEL)
        return {'x': jax.random.normal(kx, (4, 512, D_MODEL), dtype=jnp.float32), 'Wq': jax.random.normal(kq, (D_MODEL, D_MODEL), dtype=jnp.float32) * s, 'Wk': jax.random.normal(kk, (D_MODEL, D_MODEL), dtype=jnp.float32) * s, 'Wv': jax.random.normal(kv, (D_MODEL, D_MODEL), dtype=jnp.float32) * s, 'Wo': jax.random.normal(ko, (D_MODEL, D_MODEL), dtype=jnp.float32) * s}
    _L0_attn_in = _L0_attn_setup()

    def _L0_ffn_setup():
        import jax, jax.numpy as jnp
        import numpy as np
        B, S, H, I = (1, 64, 512, 1536)

        def _quantized_matmul(x, w, scale):
            wq = w.astype(jnp.float8_e4m3fn).astype(x.dtype)
            y = jnp.einsum('bsi,io->bso', x, wq)
            return y * scale
        key = jax.random.key(seed)
        ks = jax.random.split(key, 7)
        return {'x': jax.random.normal(ks[0], (B, S, H), dtype=jnp.float32), 'gate_w': jax.random.normal(ks[1], (H, I), dtype=jnp.float32) * 0.02, 'up_w': jax.random.normal(ks[2], (H, I), dtype=jnp.float32) * 0.02, 'down_w': jax.random.normal(ks[3], (I, H), dtype=jnp.float32) * 0.02, 'gate_scale': jax.random.uniform(ks[4], (I,), dtype=jnp.float32, minval=0.5, maxval=1.5), 'up_scale': jax.random.uniform(ks[5], (I,), dtype=jnp.float32, minval=0.5, maxval=1.5), 'down_scale': jax.random.uniform(ks[6], (H,), dtype=jnp.float32, minval=0.5, maxval=1.5)}
    _L0_ffn_in = _L0_ffn_setup()
    _d = {'L0_attn_x': _L0_attn_in['x'], 'L0_attn_Wq': _L0_attn_in['Wq'], 'L0_attn_Wk': _L0_attn_in['Wk'], 'L0_attn_Wv': _L0_attn_in['Wv'], 'L0_attn_Wo': _L0_attn_in['Wo'], 'L0_ffn_gate_w': _L0_ffn_in['gate_w'], 'L0_ffn_up_w': _L0_ffn_in['up_w'], 'L0_ffn_down_w': _L0_ffn_in['down_w'], 'L0_ffn_gate_scale': _L0_ffn_in['gate_scale'], 'L0_ffn_up_scale': _L0_ffn_in['up_scale'], 'L0_ffn_down_scale': _L0_ffn_in['down_scale']}
    _x0 = _d['L0_attn_x']
    _d['L0_attn_x'] = jax.random.normal(jax.random.fold_in(jax.random.key(seed), 1), (4, 1024, 512), dtype=_x0.dtype)
    del _x0
    return _d

def reference(L0_attn_x, L0_attn_Wq, L0_attn_Wk, L0_attn_Wv, L0_attn_Wo, L0_ffn_gate_w, L0_ffn_up_w, L0_ffn_down_w, L0_ffn_gate_scale, L0_ffn_up_scale, L0_ffn_down_scale):

    def _L0_attn_ref(x, Wq, Wk, Wv, Wo):
        import jax, jax.numpy as jnp
        import numpy as np
        D_MODEL = 512
        NUM_HEADS = 16
        DK = D_MODEL // NUM_HEADS
        B, S, D = x.shape
        H, dk = (NUM_HEADS, DK)
        q = (x @ Wq.T).reshape(B, S, H, dk).transpose(0, 2, 1, 3)
        k = (x @ Wk.T).reshape(B, S, H, dk).transpose(0, 2, 1, 3)
        v = (x @ Wv.T).reshape(B, S, H, dk).transpose(0, 2, 1, 3)
        scores = jnp.einsum('bhqd,bhkd->bhqk', q, k) / jnp.sqrt(jnp.float32(dk))
        causal = jnp.tril(jnp.ones((S, S), dtype=bool))
        scores = jnp.where(causal, scores, jnp.finfo(scores.dtype).min)
        probs = jax.nn.softmax(scores, axis=-1)
        attn = jnp.einsum('bhqk,bhkd->bhqd', probs, v)
        attn = attn.transpose(0, 2, 1, 3).reshape(B, S, D)
        return attn @ Wo.T

    def _L0_ffn_ref(x, gate_w, up_w, down_w, gate_scale, up_scale, down_scale):
        import jax, jax.numpy as jnp
        import numpy as np
        B, S, H, I = (1, 64, 512, 1536)

        def _quantized_matmul(x, w, scale):
            wq = w.astype(jnp.float8_e4m3fn).astype(x.dtype)
            y = jnp.einsum('bsi,io->bso', x, wq)
            return y * scale
        gate = jax.nn.silu(_quantized_matmul(x, gate_w, gate_scale))
        up = _quantized_matmul(x, up_w, up_scale)
        fuse = gate * up
        return _quantized_matmul(fuse, down_w, down_scale)
    x = L0_attn_x
    xn = _layernorm(x, axis=-1)
    x = x + _L0_attn_ref(xn, L0_attn_Wq, L0_attn_Wk, L0_attn_Wv, L0_attn_Wo) + _L0_ffn_ref(xn, L0_ffn_gate_w, L0_ffn_up_w, L0_ffn_down_w, L0_ffn_gate_scale, L0_ffn_up_scale, L0_ffn_down_scale)
    return x

_drawn_inputs = setup_inputs


def setup_inputs(seed=0):
    import zlib

    import numpy as np

    out = dict(_drawn_inputs(seed))
    spreads = {}
    factors = {}
    for name, (base, spread) in spreads.items():
        noise = np.random.default_rng([zlib.crc32(name.encode()), seed]).standard_normal(out[name].shape)
        drawn = base * np.exp(spread * noise) if base else spread * noise
        out[name] = jnp.asarray(drawn.astype(out[name].dtype))
    for name, factor in factors.items():
        out[name] = (out[name] * factor).astype(out[name].dtype)
    return out
```

```python
from contextlib import ExitStack

import concourse.bass as bass
from concourse import mybir

F32 = mybir.dt.float32
F16 = mybir.dt.float16
I32 = mybir.dt.int32
U32 = mybir.dt.uint32
ALU = mybir.AluOpType
ACT = mybir.ActivationFunctionType
AX = mybir.AxisListType
RMAX = bass.bass_isa.ReduceOp.max
ds = bass.ds

P = 128
B, S, D = 4, 1024, 512
H, DK = 16, 32
INNER = 1536
KC = D // P
FC = INNER // P
NH = B * H
TILE = 512
NT = B * S // TILE
NB = TILE // P
QB = S // P
VE = DK + 1
HI, LO = 0, 1
TERMS = ((HI, HI), (HI, LO), (LO, HI))
EPS = 1e-5
NEWTON = 3
GUESS = float(0x5F3759DF)
EXP_BITS = 0x7F800000
MSCALE = 1024.0
MASKED = -3.0e38

HEADS_PER_IT = 4
NIT = NH // HEADS_PER_IT
LAG = S // (2 * P)
FT = 2 * P

M_UNITS = ([(i, 0, (i + 1) * P, i) for i in range(4)]
           + [u for i in range(4, 8) for u in ((i, 0, 512, i), (i, 512, (i + 1) * P - 512, i + 4))])
E_UNITS = [[(0, 0, 512)], [(1, 128, 384), (3, 384, 128)], [(2, 256, 256), (6, 768, 256)],
           [(0, 512, 512)], [(1, 512, 512)], [(2, 512, 512)], [(3, 512, 512)],
           [(4, 512, 512)], [(5, 640, 384), (7, 896, 128)]]
NM, NE = len(M_UNITS), len(E_UNITS)
DIAGONAL = {0: 0, 1: 384, 2: 256, 7: 0, 8: 384}
ND = len(DIAGONAL)


def p_column(j, i):
    for u, pieces in enumerate(E_UNITS):
        at = u * 512
        for key, q0, w in pieces:
            if key == j and q0 <= i * P < q0 + w:
                return at + i * P - q0
            at += w


PV_STEP = {1: (0, 1), 2: (2,), 3: (3,), 4: (4,), 5: (5,), 6: (6,), 7: (7,)}
FFN_STEP = {k: f for f, k in enumerate((0, 2, 5, 7, 9, 12, 14, 16, 19, 21, 23, 26))}
SPLIT_STEP = {9: 0, 15: 1}
TURN_STEP = {11: 0, 16: 1}
PROJ_STEP = {13: 0, 18: 1}
DOWN_STEP = {30: (0, 0), 31: (0, 1), 33: (1, 0), 34: (1, 1)}


def wait(eng, sem, value):
    if isinstance(value, int) and value <= 0:
        return
    eng.wait_ge(sem, value)


def wait_apart(eng, sem, value, counted):
    eng.wait_ge(sem, value)
    if not isinstance(value, int):
        eng.sem_inc(counted, 1)


def prepare(nc, x, weights, ffn, scales, q_dram, k_dram, v_dram, xn_dram, keep, bank):
    wo_t, wg8, wu8, wd8, ident, s_exp, c_out, half_gs, c_ff, ds_row = (
        keep[n] for n in ("wo_t", "wg8", "wu8", "wd8", "ident", "s_exp", "c_out", "half_gs", "c_ff", "ds_row"))
    gate_w, up_w, down_w = ffn
    x_v = x.rearrange("b (u k p) d -> (b u) p k d", k=NB, p=P)
    GC = INNER // 2
    DCOL = D // NT
    gate_v = gate_w.rearrange("(k p) (h f) -> k h p f", p=P, h=2)
    up_v = up_w.rearrange("(k p) (h f) -> k h p f", p=P, h=2)
    down_v = down_w.rearrange("(c p) (t o) -> t p c o", p=P, o=DCOL)
    with ExitStack() as ctx:
        def sb(name, shape, dt):
            return ctx.enter_context(nc.sbuf_tensor(name, shape, dt))

        def sem(name):
            return ctx.enter_context(nc.semaphore(name))

        w_raw = [sb(f"w_raw{m}", [P, KC, D], F32) for m in range(4)]
        w_part = [sb(f"w_part{i}", [P, 2, KC, D], F16) for i in range(2)]
        w_t = [sb(f"w_t{m}", [P, 2, KC, D], F16) for m in range(3)] + [wo_t]
        w_max = sb("w_max", [P, 4], F32)
        w_gmax = sb("w_gmax", [P, 4], F32)
        w_pow = sb("w_pow", [P, 4], F32)
        w_inv = sb("w_inv", [P, 4], F32)
        x_in = sb("x_in", [P, NB, D], F32)
        xn = sb("xn", [P, NB, D], F32)
        x_part = sb("x_part", [P, 2, NB, D], F16)
        x_t = sb("x_t", [P, 2, KC, TILE], F16)
        stats = sb("stats", [P, NB, 6], F32)
        mv = sb("mv", [P, NB, 2], F32)
        var = sb("var", [P, NB], F32)
        rstd = sb("rstd", [P, NB], F32)
        nt0 = sb("nt0", [P, NB], F32)
        nt1 = sb("nt1", [P, NB], F32)
        qk_st = [sb(f"qk_st{i}", [P, 2, TILE], F16) for i in range(4)]
        v_st = sb("v_st", [P, H, NB, VE], F32)
        raw = sb("raw", [P, 3, GC], F32)
        cmag = sb("cmag", [P, 3, GC], F32)
        ff_max = sb("ff_max", [P, 2, NT], F32)
        ff4 = sb("ff4", [P, 4], F32)
        ff4g = sb("ff4g", [P, 4], F32)
        bound = sb("bound", [P, 4], F32)
        gs = sb("gs", [P, FC], F32)
        us = sb("us", [P, FC], F32)

        w_loaded = [sem(f"w_loaded{m}") for m in range(4)]
        small_loaded = sem("small_loaded")
        x_loaded = sem("x_loaded")
        ffw_loaded = sem("ffw_loaded")
        ident_set = sem("ident_set")
        ident_zero = sem("ident_zero")
        ones_set = sem("ones_set")
        wmax_done = sem("wmax_done")
        wgmax_done = sem("wgmax_done")
        winv_done = sem("winv_done")
        w_hi_done = sem("w_hi_done")
        w_lo_done = sem("w_lo_done")
        wt_mm = sem("wt_mm")
        wt_act = sem("wt_act")
        wt_dve = sem("wt_dve")
        ln_link = sem("ln_link")
        xn_done = sem("xn_done")
        xhi_done = sem("xhi_done")
        xlo_done = sem("xlo_done")
        xt_mm = sem("xt_mm")
        xt_act = sem("xt_act")
        xt_dve = sem("xt_dve")
        proj_mm = sem("proj_mm")
        hi_done = sem("hi_done")
        lo_done = sem("lo_done")
        v_act = sem("v_act")
        v_dve = sem("v_dve")
        qk_stored = [sem(f"qk_stored{i}") for i in range(4)]
        v_stored = sem("v_stored")
        xt_stored = sem("xt_stored")
        round_link = sem("round_link")
        rounded = sem("rounded")
        ffmax_done = sem("ffmax_done")
        ffg_done = sem("ffg_done")
        fin_link = sem("fin_link")
        waits_apart = sem("waits_apart")
        block = ctx.enter_context(nc.Block())
        LINKS = 4 + 4 * NEWTON
        ROUND_LINKS = 3

        def over_tiles(eng, tile):
            tile(0)
            with eng.Fori(1, NT - 1) as t:
                tile(t)
            tile(NT - 1)

        def has_next(t):
            return not (isinstance(t, int) and t == NT - 1)

        @block.sync
        def _(sp):
            def load_ffn_weights(t):
                for i, src in enumerate((gate_v, up_v)):
                    sp.dma_start(raw[:, i:i + 1, :],
                                 src[ds(t // 2, 1), ds(t % 2, 1)].rearrange("k h p f -> p (k h) f")
                                 ).then_inc(ffw_loaded, 16)
                sp.dma_start(raw[:, 2, :].rearrange("p (c o) -> p c o", c=FC),
                             down_v[ds(t, 1)].rearrange("a p c o -> p (a c) o")).then_inc(ffw_loaded, 16)

            sp.dma_start(x_in[:, :, :], x_v[0]).then_inc(x_loaded, 16)
            for m, w in enumerate(weights):
                sp.dma_start(w_raw[m][:, :, :], w.rearrange("(c p) k -> p c k", p=P)).then_inc(w_loaded[m], 16)
            load_ffn_weights(0)
            gate_s, up_s, down_s = scales
            with nc.allow_non_contiguous_dma(reason="two vectors of 1536 scales"):
                sp.dma_start(gs[:, :], gate_s.rearrange("(c p) -> p c", p=P)).then_inc(small_loaded, 16)
                sp.dma_start(us[:, :], up_s.rearrange("(c p) -> p c", p=P)).then_inc(small_loaded, 16)
            sp.dma_start(ds_row[:, :], down_s.rearrange("(a d) -> a d", a=1).broadcast_to([P, D])).then_inc(
                small_loaded, 16)

            def tile(t):
                if has_next(t):
                    sp.wait_ge(xn_done, t + 1)
                    sp.dma_start(x_in[:, :, :], x_v[ds(t + 1, 1)].rearrange("a p k d -> p (a k) d")
                                 ).then_inc(x_loaded, 16)
                sp.wait_ge(xt_act, 2 * t + 2)
                sp.wait_ge(xt_dve, 2 * t + 2)
                for half in range(2):
                    sp.dma_start(xn_dram[ds(2 * t + half, 1)].rearrange("a p w k t -> p (a w k) t"),
                                 x_t[:, :, :, half * FT:(half + 1) * FT].rearrange("p w k t -> p (w k) t")
                                 ).then_inc(xt_stored, 16)
                for c in range(8):
                    dst = (q_dram if c < 4 else k_dram).rearrange(
                        "w (b c a) d (u t) -> b u c (a d) w t", b=B, c=KC, u=2)
                    sp.wait_ge(lo_done, 8 * t + c + 1)
                    sp.dma_start(dst[ds(t // 2, 1), ds(t % 2, 1), c % 4].rearrange("b u p w t -> p (b u w) t"),
                                 qk_st[c % 4][:, :, :]).then_inc(qk_stored[c % 4], 16)
                sp.wait_ge(v_act, 2 * t + 2)
                sp.wait_ge(v_dve, 2 * t + 2)
                vdst = v_dram.rearrange("(b h) p (u k) e -> b u p h (k e)", b=B, u=2)
                sp.dma_start(vdst[ds(t // 2, 1), ds(t % 2, 1)].rearrange("b u p h e -> p (b u h) e"),
                             v_st[:, :, :, :].rearrange("p h k e -> p h (k e)")).then_inc(v_stored, 16)
                if has_next(t):
                    sp.wait_ge(rounded, t + 1)
                    load_ffn_weights(t + 1)

            over_tiles(sp, tile)
            for i in range(4):
                sp.wait_ge(qk_stored[i], 16 * 2 * NT)
            sp.wait_ge(v_stored, 16 * NT)
            sp.wait_ge(xt_stored, 16 * 2 * NT)

        @block.gpsimd
        def _(pool):
            nc.gpsimd.memset(ident[:, :], 0.0).then_inc(ident_zero, 1)
            pool.wait_ge(ident_zero, 1)
            nc.gpsimd.affine_select(out=ident[:, :], in_=ident[:, :], compare_op=ALU.not_equal, fill=1.0, base=0,
                                    pattern=[[-1, P]], channel_multiplier=1).then_inc(ident_set, 1)
            nc.gpsimd.memset(v_st[:, :, :, DK:VE], 1.0).then_inc(ones_set, 1)

            def x_low(t):
                pool.wait_ge(xhi_done, t + 1)
                wait(pool, xt_mm, 4 * t)
                nc.gpsimd.tensor_tensor(x_part[:, LO, :, :], xn[:, :, :], x_part[:, HI, :, :],
                                        ALU.subtract).then_inc(xlo_done, 1)

            x_low(0)
            pool.wait_ge(wmax_done, 4)
            nc.gpsimd.partition_all_reduce(w_gmax[:, :], w_max[:, :], P, RMAX).then_inc(wgmax_done, 1)
            x_low(1)
            with pool.Fori(2, NT) as t:
                x_low(t)
            pool.wait_ge(ffmax_done, 1)
            nc.gpsimd.partition_all_reduce(ff4g[:, :], ff4[:, :], P, RMAX).then_inc(ffg_done, 1)

        def pair_of_pieces(n):
            return bank[n % 2][:, :].bitcast(F16).rearrange("p (k o) -> p k o", k=2)

        @block.scalar
        def _(act):
            def x_high(t):
                act.wait_ge(xn_done, t + 1)
                wait(act, xt_mm, 4 * t)
                nc.scalar.copy(x_part[:, HI, :, :], xn[:, :, :]).then_inc(xhi_done, 1)

            def copy_weights(m):
                for n in (0, 2):
                    act.wait_ge(wt_mm, 4 * m + n + 1)
                    nc.scalar.copy(w_t[m][:, n // 2, 0:2, :], pair_of_pieces(n)).then_inc(wt_act, 1)

            x_high(0)
            act.wait_ge(winv_done, 1)
            for m in range(4):
                wait(act, wt_mm, 4 * (m - 1))
                nc.scalar.activation(w_part[m % 2][:, HI, :, :], w_raw[m][:, :, :], ACT.Copy,
                                     scale=w_inv[:, m:m + 1]).then_inc(w_hi_done, 1)
                if m >= 1:
                    copy_weights(m - 1)
            copy_weights(3)

            def tile(t):
                for n in (0, 2):
                    act.wait_ge(xt_mm, 4 * t + n + 1)
                    wait(act, xt_stored, 32 * t)
                    nc.scalar.copy(x_t[:, n // 2, 0:2, :], pair_of_pieces(n)).then_inc(xt_act, 1)
                for c in range(8):
                    act.wait_ge(proj_mm, 12 * t + c + 1)
                    wait(act, qk_stored[c % 4], 16 * (2 * t + c // 4))
                    nc.scalar.copy(qk_st[c % 4][:, HI, :], bank[2 + c % 4][:, :]).then_inc(hi_done, 1)
                    if c == 5 and has_next(t):
                        x_high(t + 1)
                for i in (0, 2):
                    act.wait_ge(proj_mm, 12 * t + 8 + i + 1)
                    wait(act, v_stored, 16 * t)
                    nc.scalar.copy(v_st[:, :, i, 0:DK],
                                   bank[2 + i][:, :].rearrange("p (h d) -> p h d", d=DK)).then_inc(v_act, 1)

            over_tiles(act, tile)

        @block.vector
        def _(dve):
            def layer_norm(t):
                done = [LINKS * t]

                def link(ins):
                    done[0] = done[0] + 1
                    ins.then_inc(ln_link, 1)
                    dve.wait_ge(ln_link, done[0])

                dve.wait_ge(x_loaded, 16 * (t + 1))
                for i in range(NB):
                    last = nc.vector.bn_stats(stats[:, i, :], x_in[:, i, :])
                last.then_inc(ln_link, 1)
                done[0] = done[0] + 1
                wait_apart(dve, ln_link, done[0], waits_apart)
                for i in range(NB):
                    last = nc.vector.bn_aggr(mv[:, i, :], stats[:, i, :])
                link(last)
                link(nc.vector.tensor_scalar(var[:, :], mv[:, :, 1], EPS, None, ALU.add))
                link(nc.vector.tensor_scalar(rstd[:, :].bitcast(I32), var[:, :].bitcast(I32), -0.5, GUESS,
                                             ALU.mult, ALU.add))
                for _ in range(NEWTON):
                    link(nc.vector.tensor_tensor(nt0[:, :], rstd[:, :], rstd[:, :], ALU.mult))
                    link(nc.vector.tensor_tensor(nt1[:, :], nt0[:, :], var[:, :], ALU.mult))
                    link(nc.vector.tensor_scalar(nt0[:, :], nt1[:, :], -0.5, 1.5, ALU.mult, ALU.add))
                    link(nc.vector.tensor_tensor(rstd[:, :], rstd[:, :], nt0[:, :], ALU.mult))
                wait(dve, xhi_done, t)
                wait(dve, xlo_done, t)
                for i in range(NB):
                    last = nc.vector.tensor_scalar(xn[:, i, :], x_in[:, i, :], mv[:, i, 0:1], rstd[:, i:i + 1],
                                                   ALU.subtract, ALU.mult)
                last.then_inc(xn_done, 1)

            def copy_weights(m):
                for n in (1, 3):
                    dve.wait_ge(wt_mm, 4 * m + n + 1)
                    nc.vector.tensor_copy(w_t[m][:, n // 2, 2:4, :], pair_of_pieces(n)).then_inc(wt_dve, 1)

            def step(ins, n):
                ins.then_inc(fin_link, 1)
                dve.wait_ge(fin_link, n)

            layer_norm(0)
            for m in range(4):
                dve.wait_ge(w_loaded[m], 16)
                nc.vector.tensor_reduce(w_max[:, m:m + 1], w_raw[m][:, :, :], AX.XY, ALU.max,
                                        apply_absolute_value=True).then_inc(wmax_done, 1)
            dve.wait_ge(wgmax_done, 1)
            step(nc.vector.tensor_scalar(w_gmax[:, :], w_gmax[:, :], 2.0 ** -50, 2.0 ** 50, ALU.max, ALU.min), 1)
            step(nc.vector.tensor_scalar(w_pow[:, :].bitcast(U32), w_gmax[:, :].bitcast(U32), EXP_BITS, None,
                                         ALU.bitwise_and), 2)
            nc.vector.reciprocal(w_inv[:, :], w_pow[:, :]).then_inc(winv_done, 1)
            step(nc.vector.tensor_tensor(s_exp[:, :], w_pow[:, 0:1], w_pow[:, 1:2], ALU.mult), 3)
            step(nc.vector.tensor_scalar(s_exp[:, :], s_exp[:, :], float(DK) ** -0.5, None, ALU.mult), 4)
            nc.vector.tensor_tensor(c_out[:, :], w_pow[:, 2:3], w_pow[:, 3:4], ALU.mult)
            dve.wait_ge(winv_done, 1)
            for m in range(4):
                dve.wait_ge(w_hi_done, m + 1)
                nc.vector.scalar_tensor_tensor(w_part[m % 2][:, LO, :, :].rearrange("p c k -> p (c k)"),
                                               w_raw[m][:, :, :].rearrange("p c k -> p (c k)"), w_inv[:, m:m + 1],
                                               w_part[m % 2][:, HI, :, :].rearrange("p c k -> p (c k)"),
                                               ALU.mult, ALU.subtract).then_inc(w_lo_done, 1)
                if m >= 1:
                    copy_weights(m - 1)
            copy_weights(3)

            def round_weights(t):
                n = ROUND_LINKS * t
                dve.wait_ge(ffw_loaded, 48 * (t + 1))
                nc.vector.tensor_reduce(ff_max[:, :, ds(t, 1)], raw[:, 0:2, :], AX.X, ALU.max,
                                        apply_absolute_value=True)
                nc.vector.tensor_scalar(cmag[:, :, :].bitcast(U32), raw[:, :, :].bitcast(U32), EXP_BITS, None,
                                        ALU.bitwise_and).then_inc(round_link, 1)
                dve.wait_ge(round_link, n + 1)
                nc.vector.tensor_scalar(cmag[:, :, :], cmag[:, :, :], 2.0 ** -6, 2.0 ** 119, ALU.max,
                                        ALU.mult).then_inc(round_link, 1)
                dve.wait_ge(round_link, n + 2)
                nc.vector.scalar_tensor_tensor(raw[:, :, :], cmag[:, :, :], 1.5 * 2.0 ** -99, raw[:, :, :],
                                               ALU.mult, ALU.add).then_inc(round_link, 1)
                dve.wait_ge(round_link, n + 3)
                for i, dst in enumerate((wg8, wu8)):
                    out = dst[:, :, :].rearrange("p k (h f) -> p (k h) f", h=2)[:, ds(t, 1), :]
                    nc.vector.scalar_tensor_tensor(out, cmag[:, i:i + 1, :], -1.5 * 2.0 ** -99, raw[:, i:i + 1, :],
                                                   ALU.mult, ALU.add)
                nc.vector.scalar_tensor_tensor(
                    wd8[:, :, ds(t * DCOL, DCOL)], cmag[:, 2, :].rearrange("p (c o) -> p c o", c=FC),
                    -1.5 * 2.0 ** -99, raw[:, 2, :].rearrange("p (c o) -> p c o", c=FC),
                    ALU.mult, ALU.add).then_inc(rounded, 1)

            def tile(t):
                for n in (1, 3):
                    dve.wait_ge(xt_mm, 4 * t + n + 1)
                    wait(dve, xt_stored, 32 * t)
                    nc.vector.tensor_copy(x_t[:, n // 2, 2:4, :], pair_of_pieces(n)).then_inc(xt_dve, 1)
                for c in range(8):
                    dve.wait_ge(hi_done, 8 * t + c + 1)
                    nc.vector.tensor_tensor(qk_st[c % 4][:, LO, :], bank[2 + c % 4][:, :], qk_st[c % 4][:, HI, :],
                                            ALU.subtract).then_inc(lo_done, 1)
                    if c == 3 and has_next(t):
                        layer_norm(t + 1)
                for i in (1, 3):
                    dve.wait_ge(proj_mm, 12 * t + 8 + i + 1)
                    wait(dve, v_stored, 16 * t)
                    nc.vector.tensor_copy(v_st[:, :, i, 0:DK],
                                          bank[2 + i][:, :].rearrange("p (h d) -> p h d", d=DK)).then_inc(v_dve, 1)
                round_weights(t)

            over_tiles(dve, tile)
            dve.wait_ge(small_loaded, 48)
            nc.vector.tensor_reduce(ff4[:, 0:2], ff_max[:, :, :], AX.X, ALU.max)
            nc.vector.tensor_reduce(ff4[:, 2:3], gs[:, :], AX.X, ALU.max, apply_absolute_value=True)
            nc.vector.tensor_reduce(ff4[:, 3:4], us[:, :], AX.X, ALU.max,
                                    apply_absolute_value=True).then_inc(ffmax_done, 1)
            dve.wait_ge(ffg_done, 1)
            step(nc.vector.tensor_scalar(bound[:, 0:2], ff4g[:, 0:2], 2.0 ** -9, 1.125 * D, ALU.add, ALU.mult), 5)
            step(nc.vector.tensor_tensor(bound[:, 0:2], bound[:, 0:2], ff4g[:, 2:4], ALU.mult), 6)
            step(nc.vector.tensor_tensor(bound[:, 2:3], bound[:, 0:1], bound[:, 1:2], ALU.mult), 7)
            step(nc.vector.tensor_scalar(bound[:, 2:3], bound[:, 2:3], 2.0 ** -50, 2.0 ** 100, ALU.max, ALU.min), 8)
            step(nc.vector.tensor_scalar(bound[:, 2:3].bitcast(U32), bound[:, 2:3].bitcast(U32), EXP_BITS, None,
                                         ALU.bitwise_and), 9)
            step(nc.vector.reciprocal(bound[:, 3:4], bound[:, 2:3]), 10)
            step(nc.vector.tensor_scalar(bound[:, 3:4], bound[:, 3:4], 2.0 ** 13, None, ALU.mult), 11)
            step(nc.vector.tensor_scalar(bound[:, 2:3], bound[:, 2:3], 2.0 ** -14, None, ALU.mult), 12)
            nc.vector.tensor_scalar(half_gs[:, :], gs[:, :], 0.5, None, ALU.mult)
            nc.vector.scalar_tensor_tensor(c_ff[:, :], gs[:, :], bound[:, 3:4], us[:, :], ALU.mult, ALU.mult)
            step(nc.vector.tensor_scalar(ds_row[:, :], ds_row[:, :], bound[:, 2:3], None, ALU.mult), 13)

        @block.tensor
        def _(pe):
            def fill(n, part, signal):
                dst = pair_of_pieces(n)
                for k in range(2):
                    for i in range(4):
                        kc = 2 * (n % 2) + k
                        mm = nc.tensor.transpose(dst[:, k, i * P:(i + 1) * P],
                                                 part[:, n // 2, i, kc * P:(kc + 1) * P], ident[:, :])
                mm.then_inc(signal, 1)

            pe.wait_ge(ident_set, 1)
            for m in range(4):
                for n in range(4):
                    pe.wait_ge(w_hi_done if n < 2 else w_lo_done, m + 1)
                    wait(pe, wt_act if n % 2 == 0 else wt_dve, 2 * m + n // 2)
                    fill(n, w_part[m % 2], wt_mm)
            pe.wait_ge(wt_act, 8)
            pe.wait_ge(wt_dve, 8)

            def tile(t):
                for n in range(4):
                    pe.wait_ge(xhi_done if n < 2 else xlo_done, t + 1)
                    wait(pe, xt_act if n % 2 == 0 else xt_dve, 2 * t + n // 2)
                    fill(n, x_part, xt_mm)
                pe.wait_ge(xt_act, 2 * t + 2)
                pe.wait_ge(xt_dve, 2 * t + 2)
                for c in range(12):
                    if c >= 4:
                        pe.wait_ge(lo_done, 8 * t + c - 3)
                    elif c % 2 == 0:
                        wait(pe, v_act, 2 * t - 1 + c // 2)
                    else:
                        wait(pe, v_dve, 2 * t - 1 + c // 2)
                    first = True
                    for wp, xp in TERMS:
                        for kc in range(KC):
                            if c < 8:
                                o = c % 4
                                lhs, rhs = w_t[c // 4][:, wp, kc, o * P:(o + 1) * P], x_t[:, xp, kc, :]
                            else:
                                i = c - 8
                                lhs, rhs = x_t[:, xp, kc, i * P:(i + 1) * P], w_t[2][:, wp, kc, :]
                            mm = nc.tensor.matmul(bank[2 + c % 4][:, :], lhs, rhs, start=first,
                                                  stop=((wp, xp) == TERMS[-1] and kc == KC - 1))
                            first = False
                    mm.then_inc(proj_mm, 1)

            over_tiles(pe, tile)


def attend(nc, x, out, q_dram, k_dram, v_dram, xn_dram, keep, bank):
    wo_t, wg8, wu8, wd8, ident, s_exp, c_out, half_gs, c_ff, ds_row = (
        keep[n] for n in ("wo_t", "wg8", "wu8", "wd8", "ident", "s_exp", "c_out", "half_gs", "c_ff", "ds_row"))
    x_v = x.rearrange("b (i p) d -> (b i) p d", p=P)
    out_v = out.rearrange("b (i p) d -> (b i) p d", p=P)
    with ExitStack() as ctx:
        def sb(name, shape, dt):
            return ctx.enter_context(nc.sbuf_tensor(name, shape, dt))

        def sem(name):
            return ctx.enter_context(nc.semaphore(name))

        q_st = [sb(f"q_st{i}", [3 * DK + 2, S], F16) for i in range(4)]
        k_st = [sb(f"k_st{i}", [3 * DK + 2, S], F16) for i in range(4)]
        v_sb = [sb(f"v_sb{i}", [P, QB, VE], F32) for i in range(4)]
        probs = [sb(f"probs{i}", [P, NE * 512], F32) for i in range(2)]
        mask = sb("mask", [P, 512], F32)
        junk = [sb(f"junk{i}", [P, 512], mybir.dt.bfloat16) for i in range(2)]
        mx = sb("mx", [P, 12], F32)
        m_part = sb("m_part", [P, 16], F16)
        m_row = [sb(f"m_row{i}", [16, P], F16) for i in range(2)]
        rsum = sb("rsum", [P, QB], F32)
        attn = sb("attn", [P, 2, QB, D], F32)
        a_part = sb("a_part", [P, 2, D], F16)
        a_t = sb("a_t", [P, 2, KC, P], F16)
        xt = sb("xt", [P, 2, KC, FT], F16)
        th = [sb(f"th{i}", [P, FT], F32) for i in range(2)]
        ga = sb("ga", [P, FT], F32)
        fu = [sb(f"fu{i}", [P, FT], F32) for i in range(2)]
        fuse = sb("fuse", [P, 2, FC, FT], F16)
        x_blk = sb("x_blk", [P, 2, D], F32)
        ff_out = sb("ff_out", [P, D], F32)
        res = sb("res", [P, QB, D], F32)
        o_sb = [sb(f"o_sb{i}", [P, D], F32) for i in range(2)]

        st_bank, m_bank = bank[0:2], bank[2:4]
        o_bank, ff_bank, misc = bank[4], bank[5:7], bank[7]
        o_all = o_bank[:, 0:QB * VE].rearrange("p (i e) -> p i e", e=VE)

        q_loaded = [sem(f"q_loaded{i}") for i in range(4)]
        v_loaded = [sem(f"v_loaded{i}") for i in range(4)]
        row_loaded = [sem(f"row_loaded{i}") for i in range(4)]
        xt_loaded = sem("xt_loaded")
        xb_loaded = sem("xb_loaded")
        out_stored = [sem(f"out_stored{i}") for i in range(2)]
        ones_set = sem("ones_set2")
        mask_zero = sem("mask_zero")
        mask_set = sem("mask_set")
        m_mm = sem("m_mm")
        m_red = sem("m_red")
        m_link = sem("m_link")
        mt_mm = sem("mt_mm")
        mt_copied = sem("mt_copied")
        e_mm = sem("e_mm")
        exp_done = sem("exp_done")
        diag_done = sem("diag_done")
        pv_mm = sem("pv_mm")
        o_link = sem("o_link")
        o_done = sem("o_done")
        ff_mm = sem("ff_mm")
        tanh_done = sem("tanh_done")
        ga_done = sem("ga_done")
        fu_done = sem("fu_done")
        fuse_hi = sem("fuse_hi")
        fuse_lo = sem("fuse_lo")
        down_mm = sem("down_mm")
        dn_link = sem("dn_link")
        res_done = sem("res_done")
        split_link = sem("split_link")
        split_done = sem("split_done")
        turn_mm = sem("turn_mm")
        turned = sem("turned")
        op_mm = sem("op_mm")
        o_ready = sem("o_ready")
        dve_waits = sem("dve_waits")
        pool_waits = sem("pool_waits")
        block = ctx.enter_context(nc.Block())

        def over_iterations(eng, step):
            step(0, False)
            with eng.Fori(1, LAG) as it:
                step(it, False)
            with eng.Fori(LAG, NIT) as it:
                step(it, True)

        def load_head(sp, n, i):
            for dst, dram, rows in ((q_st[i], q_dram, (HI, LO, HI)), (k_st[i], k_dram, (HI, HI, LO))):
                for r, w in enumerate(rows):
                    sp.dma_start(dst[r * DK:(r + 1) * DK, :], dram[w, ds(n, 1)].rearrange("a d t -> (a d) t")
                                 ).then_inc(q_loaded[i], 16)

        def load_v(sp, n, i):
            sp.dma_start(v_sb[i][:, :, :], v_dram[ds(n, 1)].rearrange("a p k e -> p (a k) e")
                         ).then_inc(v_loaded[i], 16)

        @block.sync
        def _(sp):
            def load_tile(t):
                sp.dma_start(xt[:, :, :, :].rearrange("p w k t -> p (w k) t"),
                             xn_dram[ds(t, 1)].rearrange("a p w k t -> p (a w k) t")).then_inc(xt_loaded, 16)

            def store_row(i, m):
                sp.wait_ge(mt_copied, m)
                sp.dma_start(q_st[i][3 * DK:3 * DK + 2, :], m_row[i % 2][:, :]).then_inc(row_loaded[i], 16)

            for n in range(3):
                load_head(sp, n, n)
                if n < 2:
                    load_v(sp, n, n)
            load_tile(0)
            store_row(0, 1)

            def iteration(it, with_out):
                for s in range(HEADS_PER_IT):
                    n = 4 * it + s
                    wait(sp, e_mm, NE * n)
                    load_head(sp, (n + 3) % NH, (s + 3) % 4)
                    wait(sp, pv_mm, n - 1)
                    load_v(sp, (n + 2) % NH, (s + 2) % 4)
                    if s == 2:
                        wait(sp, res_done, 2 * it)
                        sp.dma_start(x_blk[:, :, :], x_v[ds(2 * it, 2)].rearrange("a p d -> p a d")
                                     ).then_inc(xb_loaded, 16)
                        if with_out:
                            for i in range(2):
                                store_out(2 * (it - LAG) + i, i, it - LAG)
                    if s == 3:
                        sp.wait_ge(ff_mm, FC * (it + 1))
                        load_tile((it + 1) % NIT)
                    store_row((s + 1) % 4, n + 2)

            def store_out(b, i, r):
                sp.wait_ge(o_ready, 2 * r + i + 1)
                sp.dma_start(out_v[ds(b, 1)].rearrange("a p d -> p (a d)"), o_sb[i][:, :]).then_inc(out_stored[i], 16)

            over_iterations(sp, iteration)
            with sp.Fori(NIT, NIT + LAG) as it:
                for i in range(2):
                    store_out(2 * (it - LAG) + i, i, it - LAG)
            for i in range(2):
                sp.wait_ge(out_stored[i], 16 * NIT)
                sp.wait_ge(row_loaded[i], 16 * (NIT + (i == 0)))
            for i in range(4):
                sp.wait_ge(q_loaded[i], 96 * (NIT + (i < 3)))
                sp.wait_ge(v_loaded[i], 16 * (NIT + (i < 2)))
            sp.wait_ge(xt_loaded, 16 * (NIT + 1))

        @block.gpsimd
        def _(pool):
            nc.gpsimd.memset(mask[:, :], 0.0).then_inc(mask_zero, 1)
            pool.wait_ge(mask_zero, 1)
            nc.gpsimd.affine_select(out=mask[:, 512 - P:512], in_=mask[:, 512 - P:512], compare_op=ALU.is_ge,
                                    fill=MASKED, base=0, pattern=[[-1, P]], channel_multiplier=1
                                    ).then_inc(mask_set, 1)

            def low_of_fuse(g, f, it):
                pool.wait_ge(fuse_hi, g + 1)
                nc.gpsimd.tensor_tensor(fuse[:, LO, f, :], fu[f % 2][:, :], fuse[:, HI, f, :],
                                        ALU.subtract).then_inc(fuse_lo, 1)

            def iteration(it, with_out):
                for s in range(HEADS_PER_IT):
                    for u in range(NE):
                        if u in DIAGONAL:
                            wait_apart(pool, exp_done, NE * (4 * it + s) + u + 1, pool_waits)
                            blocks = 2 if DIAGONAL[u] else 1
                            step = DIAGONAL[u] or P
                            at = probs[s % 2][:, u * 512:(u + 1) * 512].rearrange("p (b q) -> p b q", q=P)
                            at = at[:, 0:(blocks - 1) * (step // P) + 1:step // P, :]
                            nc.gpsimd.affine_select(out=at, in_=at, compare_op=ALU.is_ge, fill=0.0, base=0,
                                                    pattern=[[0, blocks], [1, P]], channel_multiplier=-1
                                                    ).then_inc(diag_done, 1)
                        if s * NE + u - 1 in FFN_STEP:
                            f = FFN_STEP[s * NE + u - 1]
                            low_of_fuse(FC * it + f, f, it)

            over_iterations(pool, iteration)

        @block.scalar
        def _(act):
            def iteration(it, with_out):
                for s in range(HEADS_PER_IT):
                    n = 4 * it + s
                    for u in range(NE):
                        e = NE * n + u
                        act.wait_ge(e_mm, e + 1)
                        if u == 0:
                            wait(act, pv_mm, n - 1)
                        nc.scalar.activation(probs[s % 2][:, u * 512:(u + 1) * 512], st_bank[(s + u) % 2][:, :],
                                             ACT.Exp, scale=s_exp[:, :]).then_inc(exp_done, 1)
                        k = s * NE + u
                        if k in FFN_STEP:
                            f = FFN_STEP[k]
                            g = FC * it + f
                            act.wait_ge(ff_mm, g + 1)
                            wait(act, ga_done, g - 1)
                            nc.scalar.activation(th[f % 2][:, :], ff_bank[f % 2][:, 0:FT], ACT.Tanh,
                                                 scale=half_gs[:, f:f + 1]).then_inc(tanh_done, 1)
                        if k - 1 in FFN_STEP:
                            f = FFN_STEP[k - 1]
                            g = FC * it + f
                            act.wait_ge(fu_done, g + 1)
                            if f == 0:
                                wait(act, down_mm, 2 * it)
                            nc.scalar.copy(fuse[:, HI, f, :], fu[f % 2][:, :]).then_inc(fuse_hi, 1)

            over_iterations(act, iteration)

        @block.vector
        def _(dve):
            def row_maxima(m, units):
                for u in units:
                    i, k0, w, col = M_UNITS[u]
                    if k0 + w == (i + 1) * P:
                        wait_apart(dve, m_mm, NM * m + u + 1, dve_waits)
                    else:
                        dve.wait_ge(m_mm, NM * m + u + 1)
                    src = m_bank[u % 2][:, 0:w]
                    if k0 + w == (i + 1) * P:
                        ins = nc.vector.tensor_tensor_reduce(
                            out=junk[u % 2][:, 0:w], in0=src, in1=mask[:, 512 - w:512], scale=1.0, scalar=MASKED,
                            op0=ALU.add, op1=ALU.max, accum_out=mx[:, col:col + 1])
                    else:
                        ins = nc.vector.tensor_reduce(mx[:, col:col + 1], src, AX.X, ALU.max)
                    ins.then_inc(m_red, 1)

            def split_maxima(m):
                dve.wait_ge(m_red, NM * (m + 1))
                nc.vector.tensor_tensor(mx[:, 4:8], mx[:, 4:8], mx[:, 8:12], ALU.max).then_inc(m_link, 1)
                dve.wait_ge(m_link, 3 * m + 1)
                wait(dve, mt_mm, m)
                nc.vector.tensor_scalar(m_part[:, 0:8], mx[:, 0:8], -1.0 / MSCALE, None, ALU.mult
                                        ).then_inc(m_link, 1)
                dve.wait_ge(m_link, 3 * m + 2)
                nc.vector.scalar_tensor_tensor(m_part[:, 8:16], mx[:, 0:8], -1.0 / MSCALE, m_part[:, 0:8],
                                               ALU.mult, ALU.subtract).then_inc(m_link, 1)

            def copy_row(m, i, last_use):
                dve.wait_ge(mt_mm, m + 1)
                wait(dve, row_loaded[(i + 2) % 4], 16 * last_use)
                nc.vector.tensor_copy(m_row[i % 2][:, :], m_bank[0][0:16, 0:P // 2].bitcast(F16)
                                      ).then_inc(mt_copied, 1)

            def normalise(n, batch, head):
                dve.wait_ge(pv_mm, n + 1)
                nc.vector.reciprocal(rsum[:, :], o_all[:, :, DK]).then_inc(o_link, 1)
                dve.wait_ge(o_link, n + 1)
                dst = attn[:, ds(batch % 2, 1), :, ds(head * DK, DK)].rearrange("p a i d -> p (a i) d")
                nc.vector.tensor_tensor(dst, o_all[:, :, 0:DK],
                                        rsum[:, :].unsqueeze(2).broadcast_to([P, QB, DK]),
                                        ALU.mult).then_inc(o_done, 1)

            def split_attention(i, r):
                par, blk = (r // 4) % 2, (r % 4) * 2 + i
                src = attn[:, ds(par, 1), ds(blk, 1), :].rearrange("p a i d -> p (a i d)")
                wait(dve, turn_mm, 2 * r + i)
                nc.vector.tensor_copy(a_part[:, HI, :], src).then_inc(split_link, 1)
                dve.wait_ge(split_link, 2 * r + i + 1)
                nc.vector.tensor_tensor(a_part[:, LO, :], src, a_part[:, HI, :], ALU.subtract
                                        ).then_inc(split_done, 1)

            def copy_turned(i, r):
                dve.wait_ge(turn_mm, 2 * r + i + 1)
                nc.vector.tensor_copy(a_t[:, :, :, :].rearrange("p w k t -> p (w k t)"),
                                      misc[:, :].bitcast(F16)).then_inc(turned, 1)

            def add_output(i, r):
                dve.wait_ge(op_mm, 2 * r + i + 1)
                wait(dve, out_stored[i], 16 * r)
                blk = (r % 4) * 2 + i
                nc.vector.scalar_tensor_tensor(
                    o_sb[i][:, :], misc[:, :], c_out[:, 0:1],
                    res[:, ds(blk, 1), :].rearrange("p a d -> p (a d)"), ALU.mult, ALU.add).then_inc(o_ready, 1)

            def add_down(i, it):
                blk = (it % 4) * 2 + i
                dve.wait_ge(down_mm, 2 * it + i + 1)
                nc.vector.tensor_tensor(ff_out[:, :], misc[:, :], ds_row[:, :], ALU.mult).then_inc(dn_link, 1)
                dve.wait_ge(dn_link, 2 * it + i + 1)
                dve.wait_ge(xb_loaded, 16 * (it + 1))
                nc.vector.tensor_tensor(res[:, ds(blk, 1), :].rearrange("p a d -> p (a d)"), ff_out[:, :],
                                        x_blk[:, i, :], ALU.add).then_inc(res_done, 1)

            for i in range(4):
                last = nc.vector.memset(k_st[i][3 * DK:3 * DK + 2, :], MSCALE)
            last.then_inc(ones_set, 1)
            dve.wait_ge(mask_set, 1)
            row_maxima(0, range(NM))
            split_maxima(0)
            copy_row(0, 0, 0)

            def iteration(it, with_out):
                for s in range(HEADS_PER_IT):
                    n = 4 * it + s
                    for u in range(NE):
                        k = s * NE + u
                        if u < NM // 2:
                            row_maxima(n + 1, (2 * u, 2 * u + 1))
                        if u == NM // 2 - 1:
                            split_maxima(n + 1)
                        if u == NM // 2:
                            copy_row(n + 1, (s + 1) % 4, it if s == 0 else it + 1)
                        if k in FFN_STEP:
                            f = FFN_STEP[k]
                            g = FC * it + f
                            dve.wait_ge(tanh_done, g + 1)
                            wait(dve, fu_done, g)
                            nc.vector.scalar_tensor_tensor(ga[:, :], th[f % 2][:, :], 1.0, ff_bank[f % 2][:, 0:FT],
                                                           ALU.add, ALU.mult).then_inc(ga_done, 1)
                            dve.wait_ge(ga_done, g + 1)
                            wait(dve, fuse_lo, g - 1)
                            nc.vector.scalar_tensor_tensor(fu[f % 2][:, :], ff_bank[f % 2][:, FT:2 * FT],
                                                           c_ff[:, f:f + 1], ga[:, :], ALU.mult, ALU.mult
                                                           ).then_inc(fu_done, 1)
                        if u == NE - 1 and not (isinstance(it, int) and n == 0):
                            m = n - 1
                            normalise(m, m // H, m % H)
                        if with_out:
                            if k in SPLIT_STEP:
                                split_attention(SPLIT_STEP[k], it - LAG)
                            if k in TURN_STEP:
                                copy_turned(TURN_STEP[k], it - LAG)
                            if k in PROJ_STEP:
                                add_output(PROJ_STEP[k], it - LAG)
                        if k in DOWN_STEP and DOWN_STEP[k][1] == 1:
                            add_down(DOWN_STEP[k][0], it)

            over_iterations(dve, iteration)
            normalise(NH - 1, B - 1, H - 1)
            dve.wait_ge(o_done, NH)
            with dve.Fori(NIT, NIT + LAG) as it:
                for i in range(2):
                    split_attention(i, it - LAG)
                    copy_turned(i, it - LAG)
                    add_output(i, it - LAG)

        @block.tensor
        def _(pe):
            def maxima_scores(m, i, units):
                rows = slice(0, 3 * DK)
                for u in units:
                    blk, k0, w, _ = M_UNITS[u]
                    wait(pe, m_red, NM * m + u - 1)
                    if u == 0:
                        wait(pe, mt_copied, m)
                    nc.tensor.matmul(m_bank[u % 2][:, 0:w], q_st[i][rows, blk * P:(blk + 1) * P],
                                     k_st[i][rows, k0:k0 + w], start=True, stop=True).then_inc(m_mm, 1)

            def turn_maxima(m):
                pe.wait_ge(m_link, 3 * (m + 1))
                nc.tensor.transpose(m_bank[0][0:16, 0:P // 2].bitcast(F16), m_part[:, :], ident[:, :]
                                    ).then_inc(mt_mm, 1)

            def scores(n, s, u):
                e = NE * n + u
                wait(pe, exp_done, e - 1)
                at = 0
                for j, q0, w in E_UNITS[u]:
                    mm = nc.tensor.matmul(st_bank[(s + u) % 2][:, at:at + w], k_st[s][:, j * P:(j + 1) * P],
                                          q_st[s][:, q0:q0 + w], start=True, stop=True)
                    at += w
                mm.then_inc(e_mm, 1)

            def values(s, i):
                for j in range(i + 1):
                    at = p_column(j, i)
                    mm = nc.tensor.matmul(o_all[:, i, :], probs[s % 2][:, at:at + P], v_sb[s][:, j, :],
                                          start=(j == 0), stop=(j == i))
                if i == QB - 1:
                    mm.then_inc(pv_mm, 1)

            def start_values(n, s, uses):
                pe.wait_ge(exp_done, NE * (n + 1))
                pe.wait_ge(diag_done, ND * (n + 1))
                pe.wait_ge(v_loaded[s], 16 * uses)
                wait(pe, o_done, n)

            def feed_forward(g, f, it):
                if f == 0:
                    pe.wait_ge(xt_loaded, 16 * (it + 1))
                wait(pe, fu_done, g - 1)
                for h, w8 in enumerate((wg8, wu8)):
                    for part in (HI, LO):
                        for kc in range(KC):
                            mm = nc.tensor.matmul(ff_bank[f % 2][:, h * FT:(h + 1) * FT],
                                                  w8[:, kc, f * P:(f + 1) * P], xt[:, part, kc, :],
                                                  start=(part == HI and kc == 0), stop=(part == LO and kc == KC - 1))
                mm.then_inc(ff_mm, 1)

            def down(i, half, it, with_out):
                if half == 0:
                    pe.wait_ge(fuse_lo, FC * (it + 1))
                    if i == 1 or not with_out:
                        wait(pe, res_done, 2 * it + i)
                    else:
                        pe.wait_ge(o_ready, 2 * (it - LAG) + 2)
                for f in range(half * FC // 2, (half + 1) * FC // 2):
                    for part in (HI, LO):
                        mm = nc.tensor.matmul(misc[:, :], fuse[:, part, f, i * P:(i + 1) * P], wd8[:, f, :],
                                              start=(f == 0 and part == HI), stop=(f == FC - 1 and part == LO))
                if half == 1:
                    mm.then_inc(down_mm, 1)

            def turn_attention(i, r, after_down):
                pe.wait_ge(split_done, 2 * r + i + 1)
                if i == 1:
                    pe.wait_ge(o_ready, 2 * r + 1)
                elif after_down is not None:
                    pe.wait_ge(res_done, after_down)
                else:
                    pe.wait_ge(res_done, 2 * NIT)
                    wait(pe, o_ready, 2 * r)
                dst = misc[:, :].bitcast(F16).rearrange("p (w k t) -> p w k t", w=2, k=KC)
                for part in (HI, LO):
                    for kc in range(KC):
                        mm = nc.tensor.transpose(dst[:, part, kc, :], a_part[:, part, kc * P:(kc + 1) * P],
                                                 ident[:, :])
                mm.then_inc(turn_mm, 1)

            def project(i, r):
                pe.wait_ge(turned, 2 * r + i + 1)
                for ap, wp in TERMS:
                    for kc in range(KC):
                        mm = nc.tensor.matmul(misc[:, :], a_t[:, ap, kc, :], wo_t[:, wp, kc, :],
                                              start=((ap, wp) == TERMS[0] and kc == 0),
                                              stop=((ap, wp) == TERMS[-1] and kc == KC - 1))
                mm.then_inc(op_mm, 1)

            pe.wait_ge(ones_set, 1)
            pe.wait_ge(q_loaded[0], 96)
            maxima_scores(0, 0, range(NM))
            turn_maxima(0)

            def iteration(it, with_out):
                for s in range(HEADS_PER_IT):
                    n = 4 * it + s
                    for u in range(NE):
                        k = s * NE + u
                        if u == 0:
                            pe.wait_ge(q_loaded[(s + 1) % 4], 96 * ((it + 1) if s < 3 else (it + 2)))
                        if u < NM // 2:
                            maxima_scores(n + 1, (s + 1) % 4, (2 * u, 2 * u + 1))
                        if u == 0:
                            pe.wait_ge(row_loaded[s], 16 * (it + 1))
                        scores(n, s, u)
                        if not (isinstance(it, int) and n == 0):
                            if u == 1:
                                start_values(n - 1, (s + 3) % 4, it if s == 0 else it + 1)
                            for i in PV_STEP.get(u, ()):
                                values((s + 3) % 4, i)
                        if u == NM // 2:
                            turn_maxima(n + 1)
                        if k in FFN_STEP:
                            feed_forward(FC * it + FFN_STEP[k], FFN_STEP[k], it)
                        if with_out:
                            if k in TURN_STEP:
                                turn_attention(TURN_STEP[k], it - LAG, 2 * it)
                            if k in PROJ_STEP:
                                project(PROJ_STEP[k], it - LAG)
                        if k in DOWN_STEP:
                            down(*DOWN_STEP[k], it, with_out)

            over_iterations(pe, iteration)
            start_values(NH - 1, 3, NIT)
            for i in range(QB):
                values(3, i)
            with pe.Fori(NIT, NIT + LAG) as it:
                for i in range(2):
                    turn_attention(i, it - LAG, None)
                    project(i, it - LAG)


def build(nc, x, wq, wk, wv, wo, gate_w, up_w, down_w, gate_s, up_s, down_s, out):
    q_dram = nc.dram_tensor("q_parts", (2, NH, DK, S), F16, kind="Internal").ap()
    k_dram = nc.dram_tensor("k_parts", (2, NH, DK, S), F16, kind="Internal").ap()
    v_dram = nc.dram_tensor("v_ones", (NH, P, QB, VE), F32, kind="Internal").ap()
    xn_dram = nc.dram_tensor("xn_parts", (NIT, P, 2, KC, FT), F16, kind="Internal").ap()
    with ExitStack() as ctx:
        def sb(name, shape, dt):
            return ctx.enter_context(nc.sbuf_tensor(name, shape, dt))

        bank = [ctx.enter_context(nc.psum_tensor(f"bank{i}", [P, 512], F32)) for i in range(8)]
        keep = {"wo_t": sb("wo_t", [P, 2, KC, D], F16), "wg8": sb("wg8", [P, KC, INNER], F16),
                "wu8": sb("wu8", [P, KC, INNER], F16), "wd8": sb("wd8", [P, FC, D], F16),
                "ident": sb("ident", [P, P], F16), "s_exp": sb("s_exp", [P, 1], F32),
                "c_out": sb("c_out", [P, 1], F32), "half_gs": sb("half_gs", [P, FC], F32),
                "c_ff": sb("c_ff", [P, FC], F32), "ds_row": sb("ds_row", [P, D], F32)}
        prepare(nc, x, (wq, wk, wv, wo), (gate_w, up_w, down_w), (gate_s, up_s, down_s),
                q_dram, k_dram, v_dram, xn_dram, keep, bank)
        attend(nc, x, out, q_dram, k_dram, v_dram, xn_dram, keep, bank)


_INS = ["L0_attn_x", "L0_attn_Wq", "L0_attn_Wk", "L0_attn_Wv", "L0_attn_Wo", "L0_ffn_gate_w", "L0_ffn_up_w",
        "L0_ffn_down_w", "L0_ffn_gate_scale", "L0_ffn_up_scale", "L0_ffn_down_scale"]


def kernel(**inputs):
    import numpy as _np
    import concourse.bacc as _bacc
    from concourse import mybir as _mybir
    from concourse.bass_utils import run_bass_kernel_spmd as _run

    nc = _bacc.Bacc("TRN2", target_bir_lowering=False, num_devices=1)
    arrays, args = {}, []
    for name in _INS:
        a = _np.ascontiguousarray(inputs[name])
        arrays[f"in_{name}"] = a
        args.append(nc.dram_tensor(f"in_{name}", a.shape, _mybir.dt.from_np(a.dtype), kind="ExternalInput").ap())
    args.append(nc.dram_tensor("out_0", (B, S, D), F32, kind="ExternalOutput").ap())
    build(nc, *args)
    r = _run(nc, [arrays], core_ids=[0])
    return r.results[0]["out_0"]
```

```python
from contextlib import ExitStack

import concourse.bass as bass
from concourse import mybir

F32 = mybir.dt.float32
F16 = mybir.dt.float16
I32 = mybir.dt.int32
U32 = mybir.dt.uint32
ALU = mybir.AluOpType
ACT = mybir.ActivationFunctionType
AX = mybir.AxisListType
RMAX = bass.bass_isa.ReduceOp.max
ds = bass.ds

P = 128
B, S, D = 4, 1024, 512
H, DK = 16, 32
INNER = 1536
KC = D // P
FC = INNER // P
NH = B * H
TILE = 512
NT = B * S // TILE
NB = TILE // P
QB = S // P
VE = 2 * DK + 2
VN = 2 * DK + 1
HI, LO = 0, 1
TERMS = ((HI, HI), (HI, LO), (LO, HI))
EPS = 1e-5
NEWTON = 3
GUESS = float(0x5F3759DF)
EXP_BITS = 0x7F800000
MSCALE = 1024.0
MASKED = -3.0e38

HEADS_PER_IT = 4
NIT = NH // HEADS_PER_IT
LAG = S // (2 * P)
FT = 2 * P

M_UNITS = ([(i, 0, (i + 1) * P, i) for i in range(4)]
           + [u for i in range(4, 8) for u in ((i, 0, 512, i), (i, 512, (i + 1) * P - 512, i + 4))])
E_UNITS = [[(0, 0, 512)], [(1, 128, 384), (3, 384, 128)], [(2, 256, 256), (6, 768, 256)],
           [(0, 512, 512)], [(1, 512, 512)], [(2, 512, 512)], [(3, 512, 512)],
           [(4, 512, 512)], [(5, 640, 384), (7, 896, 128)]]
NM, NE = len(M_UNITS), len(E_UNITS)
DIAGONAL = {0: 0, 1: 384, 2: 256, 7: 0, 8: 384}
ND = len(DIAGONAL)


def p_column(j, i):
    for u, pieces in enumerate(E_UNITS):
        at = u * 512
        for key, q0, w in pieces:
            if key == j and q0 <= i * P < q0 + w:
                return at + i * P - q0
            at += w


POOL_LOW = (2, 3, 4, 5, 6, 7)
DVE_LOW = tuple(u for u in range(NE) if u not in POOL_LOW)
RING = 6
STEPS = HEADS_PER_IT * NE


def low_parts(units, k):
    return len(units) * (k // NE) + sum(u <= k % NE for u in units)


M_STEP = {1: (0, 1), 2: (2,), 3: (3, 4), 4: (5,), 5: (6, 7), 6: (8,), 7: (9, 10), 8: (11,)}
PV_STEP = {1: (0, 1), 2: (2,), 3: (3,), 5: (4,), 6: (5,), 7: (6,), 8: (7,)}
ROW_STEP = 5
DOWN_STEP = {0: (0, 0), 1: (0, 1), 2: (1, 0), 3: (1, 1)}
ADD_DOWN_STEP = {2: 0, 4: 1}
FFN_STEP = {k: f for f, k in enumerate((4, 6, 8, 10, 14, 16, 21, 23, 25, 27, 29, 31))}
SPLIT_STEP = {9: 0, 15: 1}
TURN_STEP = {10: 0, 16: 1}
PROJ_STEP = {11: (0, 0), 12: (0, 1), 18: (1, 0), 19: (1, 1)}
ADD_OUT_STEP = {13: 0, 20: 1}


def wait(eng, sem, value):
    if isinstance(value, int) and value <= 0:
        return
    eng.wait_ge(sem, value)


def wait_apart(eng, sem, value, counted):
    eng.wait_ge(sem, value)
    if not isinstance(value, int):
        eng.sem_inc(counted, 1)


def prepare(nc, x, weights, ffn, scales, q_dram, k_dram, v_dram, xn_dram, keep, bank):
    wo_t, wg8, wu8, wd8, ident, s_exp, c_out, half_gs, c_ff, ds_row = (
        keep[n] for n in ("wo_t", "wg8", "wu8", "wd8", "ident", "s_exp", "c_out", "half_gs", "c_ff", "ds_row"))
    gate_w, up_w, down_w = ffn
    x_v = x.rearrange("b (u k p) d -> (b u) p k d", k=NB, p=P)
    GC = INNER // 2
    DCOL = D // NT
    gate_v = gate_w.rearrange("(k p) (h f) -> k h p f", p=P, h=2)
    up_v = up_w.rearrange("(k p) (h f) -> k h p f", p=P, h=2)
    down_v = down_w.rearrange("(c p) (t o) -> t p c o", p=P, o=DCOL)
    with ExitStack() as ctx:
        def sb(name, shape, dt):
            return ctx.enter_context(nc.sbuf_tensor(name, shape, dt))

        def sem(name):
            return ctx.enter_context(nc.semaphore(name))

        w_raw = [sb(f"w_raw{m}", [P, KC, D], F32) for m in range(4)]
        w_part = [sb(f"w_part{i}", [P, 2, KC, D], F16) for i in range(2)]
        w_t = [sb(f"w_t{m}", [P, 2, KC, D], F16) for m in range(3)] + [wo_t]
        w_max = sb("w_max", [P, 4], F32)
        w_gmax = sb("w_gmax", [P, 4], F32)
        w_pow = sb("w_pow", [P, 4], F32)
        w_inv = sb("w_inv", [P, 4], F32)
        x_in = sb("x_in", [P, NB, D], F32)
        xn = sb("xn", [P, NB, D], F32)
        x_part = sb("x_part", [P, 2, NB, D], F16)
        x_t = sb("x_t", [P, 2, KC, TILE], F16)
        stats = sb("stats", [P, NB, 6], F32)
        mv = sb("mv", [P, NB, 2], F32)
        var = sb("var", [P, NB], F32)
        rstd = sb("rstd", [P, NB], F32)
        nt0 = sb("nt0", [P, NB], F32)
        nt1 = sb("nt1", [P, NB], F32)
        qk_st = [sb(f"qk_st{i}", [P, 2, TILE], F16) for i in range(4)]
        v_st = sb("v_st", [P, H, NB, VE], F16)
        raw = sb("raw", [P, 3, GC], F32)
        cmag = sb("cmag", [P, 3, GC], F32)
        ff_max = sb("ff_max", [P, 2, NT], F32)
        ff4 = sb("ff4", [P, 4], F32)
        ff4g = sb("ff4g", [P, 4], F32)
        bound = sb("bound", [P, 4], F32)
        gs = sb("gs", [P, FC], F32)
        us = sb("us", [P, FC], F32)

        w_loaded = [sem(f"w_loaded{m}") for m in range(4)]
        small_loaded = sem("small_loaded")
        x_loaded = sem("x_loaded")
        ffw_loaded = sem("ffw_loaded")
        ident_set = sem("ident_set")
        ident_zero = sem("ident_zero")
        ones_set = sem("ones_set")
        wmax_done = sem("wmax_done")
        wgmax_done = sem("wgmax_done")
        winv_done = sem("winv_done")
        w_hi_done = sem("w_hi_done")
        w_lo_done = sem("w_lo_done")
        wt_mm = sem("wt_mm")
        wt_act = sem("wt_act")
        wt_dve = sem("wt_dve")
        ln_link = sem("ln_link")
        xn_done = sem("xn_done")
        xhi_done = sem("xhi_done")
        xlo_done = sem("xlo_done")
        xt_mm = sem("xt_mm")
        xt_act = sem("xt_act")
        xt_dve = sem("xt_dve")
        proj_mm = sem("proj_mm")
        hi_done = sem("hi_done")
        lo_done = sem("lo_done")
        qk_stored = [sem(f"qk_stored{i}") for i in range(4)]
        v_stored = sem("v_stored")
        xt_stored = sem("xt_stored")
        round_link = sem("round_link")
        rounded = sem("rounded")
        ffmax_done = sem("ffmax_done")
        ffg_done = sem("ffg_done")
        fin_link = sem("fin_link")
        waits_apart = sem("waits_apart")
        block = ctx.enter_context(nc.Block())
        LINKS = 4 + 4 * NEWTON
        ROUND_LINKS = 3

        def over_tiles(eng, tile):
            tile(0)
            with eng.Fori(1, NT - 1) as t:
                tile(t)
            tile(NT - 1)

        def has_next(t):
            return not (isinstance(t, int) and t == NT - 1)

        @block.sync
        def _(sp):
            def load_ffn_weights(t):
                for i, src in enumerate((gate_v, up_v)):
                    sp.dma_start(raw[:, i:i + 1, :],
                                 src[ds(t // 2, 1), ds(t % 2, 1)].rearrange("k h p f -> p (k h) f")
                                 ).then_inc(ffw_loaded, 16)
                sp.dma_start(raw[:, 2, :].rearrange("p (c o) -> p c o", c=FC),
                             down_v[ds(t, 1)].rearrange("a p c o -> p (a c) o")).then_inc(ffw_loaded, 16)

            sp.dma_start(x_in[:, :, :], x_v[0]).then_inc(x_loaded, 16)
            for m, w in enumerate(weights):
                sp.dma_start(w_raw[m][:, :, :], w.rearrange("(c p) k -> p c k", p=P)).then_inc(w_loaded[m], 16)
            load_ffn_weights(0)
            gate_s, up_s, down_s = scales
            with nc.allow_non_contiguous_dma(reason="two vectors of 1536 scales"):
                sp.dma_start(gs[:, :], gate_s.rearrange("(c p) -> p c", p=P)).then_inc(small_loaded, 16)
                sp.dma_start(us[:, :], up_s.rearrange("(c p) -> p c", p=P)).then_inc(small_loaded, 16)
            sp.dma_start(ds_row[:, :], down_s.rearrange("(a d) -> a d", a=1).broadcast_to([P, D])).then_inc(
                small_loaded, 16)

            def tile(t):
                if has_next(t):
                    sp.wait_ge(xn_done, t + 1)
                    sp.dma_start(x_in[:, :, :], x_v[ds(t + 1, 1)].rearrange("a p k d -> p (a k) d")
                                 ).then_inc(x_loaded, 16)
                sp.wait_ge(xt_act, 2 * t + 2)
                sp.wait_ge(xt_dve, 2 * t + 2)
                for half in range(2):
                    sp.dma_start(xn_dram[ds(2 * t + half, 1)].rearrange("a p w k t -> p (a w k) t"),
                                 x_t[:, :, :, half * FT:(half + 1) * FT].rearrange("p w k t -> p (w k) t")
                                 ).then_inc(xt_stored, 16)
                for c in range(8):
                    dst = (q_dram if c < 4 else k_dram).rearrange(
                        "w (b c a) d (u t) -> b u c (a d) w t", b=B, c=KC, u=2)
                    sp.wait_ge(lo_done, 12 * t + c + 1)
                    sp.dma_start(dst[ds(t // 2, 1), ds(t % 2, 1), c % 4].rearrange("b u p w t -> p (b u w) t"),
                                 qk_st[c % 4][:, :, :]).then_inc(qk_stored[c % 4], 16)
                sp.wait_ge(lo_done, 12 * t + 12)
                vdst = v_dram.rearrange("(b h) p (u k) e -> b u p h (k e)", b=B, u=2)
                sp.dma_start(vdst[ds(t // 2, 1), ds(t % 2, 1)].rearrange("b u p h e -> p (b u h) e"),
                             v_st[:, :, :, :].rearrange("p h k e -> p h (k e)")).then_inc(v_stored, 16)
                if has_next(t):
                    sp.wait_ge(rounded, t + 1)
                    load_ffn_weights(t + 1)

            over_tiles(sp, tile)
            for i in range(4):
                sp.wait_ge(qk_stored[i], 16 * 2 * NT)
            sp.wait_ge(v_stored, 16 * NT)
            sp.wait_ge(xt_stored, 16 * 2 * NT)

        @block.gpsimd
        def _(pool):
            nc.gpsimd.memset(ident[:, :], 0.0).then_inc(ident_zero, 1)
            pool.wait_ge(ident_zero, 1)
            nc.gpsimd.affine_select(out=ident[:, :], in_=ident[:, :], compare_op=ALU.not_equal, fill=1.0, base=0,
                                    pattern=[[-1, P]], channel_multiplier=1).then_inc(ident_set, 1)
            nc.gpsimd.memset(v_st[:, :, :, 2 * DK:VE], 1.0).then_inc(ones_set, 1)

            def x_low(t):
                pool.wait_ge(xhi_done, t + 1)
                wait(pool, xt_mm, 4 * t)
                nc.gpsimd.tensor_tensor(x_part[:, LO, :, :], xn[:, :, :], x_part[:, HI, :, :],
                                        ALU.subtract).then_inc(xlo_done, 1)

            x_low(0)
            pool.wait_ge(wmax_done, 4)
            nc.gpsimd.partition_all_reduce(w_gmax[:, :], w_max[:, :], P, RMAX).then_inc(wgmax_done, 1)
            x_low(1)
            with pool.Fori(2, NT) as t:
                x_low(t)
            pool.wait_ge(ffmax_done, 1)
            nc.gpsimd.partition_all_reduce(ff4g[:, :], ff4[:, :], P, RMAX).then_inc(ffg_done, 1)

        def pair_of_pieces(n):
            return bank[(0, 1, 6, 7)[n]][:, :].bitcast(F16).rearrange("p (k o) -> p k o", k=2)

        @block.scalar
        def _(act):
            def x_high(t):
                act.wait_ge(xn_done, t + 1)
                wait(act, xt_mm, 4 * t)
                nc.scalar.copy(x_part[:, HI, :, :], xn[:, :, :]).then_inc(xhi_done, 1)

            def copy_weights(m):
                for n in (0, 2):
                    act.wait_ge(wt_mm, 4 * m + n + 1)
                    nc.scalar.copy(w_t[m][:, n // 2, 0:2, :], pair_of_pieces(n)).then_inc(wt_act, 1)

            x_high(0)
            act.wait_ge(winv_done, 1)
            for m in range(4):
                wait(act, wt_mm, 4 * (m - 1))
                nc.scalar.activation(w_part[m % 2][:, HI, :, :], w_raw[m][:, :, :], ACT.Copy,
                                     scale=w_inv[:, m:m + 1]).then_inc(w_hi_done, 1)
                if m >= 1:
                    copy_weights(m - 1)
            copy_weights(3)

            def tile(t):
                for n in (0, 2):
                    act.wait_ge(xt_mm, 4 * t + n + 1)
                    wait(act, xt_stored, 32 * t)
                    nc.scalar.copy(x_t[:, n // 2, 0:2, :], pair_of_pieces(n)).then_inc(xt_act, 1)
                for c in range(8):
                    act.wait_ge(proj_mm, 12 * t + c + 1)
                    wait(act, qk_stored[c % 4], 16 * (2 * t + c // 4))
                    nc.scalar.copy(qk_st[c % 4][:, HI, :], bank[2 + c % 4][:, :]).then_inc(hi_done, 1)
                    if c == 5 and has_next(t):
                        x_high(t + 1)
                for i in range(NB):
                    act.wait_ge(proj_mm, 12 * t + 8 + i + 1)
                    wait(act, v_stored, 16 * t)
                    nc.scalar.copy(v_st[:, :, i, DK:2 * DK],
                                   bank[2 + i][:, :].rearrange("p (h d) -> p h d", d=DK)).then_inc(hi_done, 1)

            over_tiles(act, tile)

        @block.vector
        def _(dve):
            def layer_norm(t):
                done = [LINKS * t]

                def link(ins):
                    done[0] = done[0] + 1
                    ins.then_inc(ln_link, 1)
                    dve.wait_ge(ln_link, done[0])

                dve.wait_ge(x_loaded, 16 * (t + 1))
                for i in range(NB):
                    last = nc.vector.bn_stats(stats[:, i, :], x_in[:, i, :])
                last.then_inc(ln_link, 1)
                done[0] = done[0] + 1
                wait_apart(dve, ln_link, done[0], waits_apart)
                for i in range(NB):
                    last = nc.vector.bn_aggr(mv[:, i, :], stats[:, i, :])
                link(last)
                link(nc.vector.tensor_scalar(var[:, :], mv[:, :, 1], EPS, None, ALU.add))
                link(nc.vector.tensor_scalar(rstd[:, :].bitcast(I32), var[:, :].bitcast(I32), -0.5, GUESS,
                                             ALU.mult, ALU.add))
                for _ in range(NEWTON):
                    link(nc.vector.tensor_tensor(nt0[:, :], rstd[:, :], rstd[:, :], ALU.mult))
                    link(nc.vector.tensor_tensor(nt1[:, :], nt0[:, :], var[:, :], ALU.mult))
                    link(nc.vector.tensor_scalar(nt0[:, :], nt1[:, :], -0.5, 1.5, ALU.mult, ALU.add))
                    link(nc.vector.tensor_tensor(rstd[:, :], rstd[:, :], nt0[:, :], ALU.mult))
                wait(dve, xhi_done, t)
                wait(dve, xlo_done, t)
                for i in range(NB):
                    last = nc.vector.tensor_scalar(xn[:, i, :], x_in[:, i, :], mv[:, i, 0:1], rstd[:, i:i + 1],
                                                   ALU.subtract, ALU.mult)
                last.then_inc(xn_done, 1)

            def copy_weights(m):
                for n in (1, 3):
                    dve.wait_ge(wt_mm, 4 * m + n + 1)
                    nc.vector.tensor_copy(w_t[m][:, n // 2, 2:4, :], pair_of_pieces(n)).then_inc(wt_dve, 1)

            def step(ins, n):
                ins.then_inc(fin_link, 1)
                dve.wait_ge(fin_link, n)

            layer_norm(0)
            for m in range(4):
                dve.wait_ge(w_loaded[m], 16)
                nc.vector.tensor_reduce(w_max[:, m:m + 1], w_raw[m][:, :, :], AX.XY, ALU.max,
                                        apply_absolute_value=True).then_inc(wmax_done, 1)
            dve.wait_ge(wgmax_done, 1)
            step(nc.vector.tensor_scalar(w_gmax[:, :], w_gmax[:, :], 2.0 ** -50, 2.0 ** 50, ALU.max, ALU.min), 1)
            step(nc.vector.tensor_scalar(w_pow[:, :].bitcast(U32), w_gmax[:, :].bitcast(U32), EXP_BITS, None,
                                         ALU.bitwise_and), 2)
            nc.vector.reciprocal(w_inv[:, :], w_pow[:, :]).then_inc(winv_done, 1)
            step(nc.vector.tensor_tensor(s_exp[:, :], w_pow[:, 0:1], w_pow[:, 1:2], ALU.mult), 3)
            step(nc.vector.tensor_scalar(s_exp[:, :], s_exp[:, :], float(DK) ** -0.5, None, ALU.mult), 4)
            nc.vector.tensor_tensor(c_out[:, :], w_pow[:, 2:3], w_pow[:, 3:4], ALU.mult)
            dve.wait_ge(winv_done, 1)
            for m in range(4):
                dve.wait_ge(w_hi_done, m + 1)
                nc.vector.scalar_tensor_tensor(w_part[m % 2][:, LO, :, :].rearrange("p c k -> p (c k)"),
                                               w_raw[m][:, :, :].rearrange("p c k -> p (c k)"), w_inv[:, m:m + 1],
                                               w_part[m % 2][:, HI, :, :].rearrange("p c k -> p (c k)"),
                                               ALU.mult, ALU.subtract).then_inc(w_lo_done, 1)
                if m >= 1:
                    copy_weights(m - 1)
            copy_weights(3)

            def round_weights(t, i):
                n = 3 * ROUND_LINKS * t + ROUND_LINKS * i
                part, mag = raw[:, i:i + 1, :], cmag[:, i:i + 1, :]
                dve.wait_ge(ffw_loaded, 48 * (t + 1))
                if i < 2:
                    nc.vector.tensor_reduce(ff_max[:, i, ds(t, 1)], part, AX.XY, ALU.max, apply_absolute_value=True)
                nc.vector.tensor_scalar(mag.bitcast(U32), part.bitcast(U32), EXP_BITS, None, ALU.bitwise_and
                                        ).then_inc(round_link, 1)
                dve.wait_ge(round_link, n + 1)
                nc.vector.tensor_scalar(mag, mag, 2.0 ** -6, 2.0 ** 119, ALU.max, ALU.mult).then_inc(round_link, 1)
                dve.wait_ge(round_link, n + 2)
                nc.vector.scalar_tensor_tensor(part, mag, 1.5 * 2.0 ** -99, part, ALU.mult, ALU.add
                                               ).then_inc(round_link, 1)
                dve.wait_ge(round_link, n + 3)
                if i < 2:
                    dst = (wg8, wu8)[i][:, :, :].rearrange("p k (h f) -> p (k h) f", h=2)[:, ds(t, 1), :]
                    nc.vector.scalar_tensor_tensor(dst, mag, -1.5 * 2.0 ** -99, part, ALU.mult, ALU.add)
                else:
                    nc.vector.scalar_tensor_tensor(
                        wd8[:, :, ds(t * DCOL, DCOL)], cmag[:, 2, :].rearrange("p (c o) -> p c o", c=FC),
                        -1.5 * 2.0 ** -99, raw[:, 2, :].rearrange("p (c o) -> p c o", c=FC),
                        ALU.mult, ALU.add).then_inc(rounded, 1)

            def tile(t):
                for n in (1, 3):
                    dve.wait_ge(xt_mm, 4 * t + n + 1)
                    wait(dve, xt_stored, 32 * t)
                    nc.vector.tensor_copy(x_t[:, n // 2, 2:4, :], pair_of_pieces(n)).then_inc(xt_dve, 1)
                for c in range(12):
                    dve.wait_ge(hi_done, 12 * t + c + 1)
                    src = bank[2 + c % 4][:, :]
                    if c < 8:
                        nc.vector.tensor_tensor(qk_st[c % 4][:, LO, :], src, qk_st[c % 4][:, HI, :],
                                                ALU.subtract).then_inc(lo_done, 1)
                    else:
                        at = v_st[:, :, c - 8, :]
                        nc.vector.tensor_tensor(at[:, :, 0:DK], src.rearrange("p (h d) -> p h d", d=DK),
                                                at[:, :, DK:2 * DK], ALU.subtract).then_inc(lo_done, 1)
                    if c == 1 and has_next(t):
                        layer_norm(t + 1)
                    if 4 <= c < 7:
                        round_weights(t, c - 4)

            over_tiles(dve, tile)
            dve.wait_ge(small_loaded, 48)
            nc.vector.tensor_reduce(ff4[:, 0:2], ff_max[:, :, :], AX.X, ALU.max)
            nc.vector.tensor_reduce(ff4[:, 2:3], gs[:, :], AX.X, ALU.max, apply_absolute_value=True)
            nc.vector.tensor_reduce(ff4[:, 3:4], us[:, :], AX.X, ALU.max,
                                    apply_absolute_value=True).then_inc(ffmax_done, 1)
            dve.wait_ge(ffg_done, 1)
            step(nc.vector.tensor_scalar(bound[:, 0:2], ff4g[:, 0:2], 2.0 ** -9, 1.125 * D, ALU.add, ALU.mult), 5)
            step(nc.vector.tensor_tensor(bound[:, 0:2], bound[:, 0:2], ff4g[:, 2:4], ALU.mult), 6)
            step(nc.vector.tensor_tensor(bound[:, 2:3], bound[:, 0:1], bound[:, 1:2], ALU.mult), 7)
            step(nc.vector.tensor_scalar(bound[:, 2:3], bound[:, 2:3], 2.0 ** -50, 2.0 ** 100, ALU.max, ALU.min), 8)
            step(nc.vector.tensor_scalar(bound[:, 2:3].bitcast(U32), bound[:, 2:3].bitcast(U32), EXP_BITS, None,
                                         ALU.bitwise_and), 9)
            step(nc.vector.reciprocal(bound[:, 3:4], bound[:, 2:3]), 10)
            step(nc.vector.tensor_scalar(bound[:, 3:4], bound[:, 3:4], 2.0 ** 13, None, ALU.mult), 11)
            step(nc.vector.tensor_scalar(bound[:, 2:3], bound[:, 2:3], 2.0 ** -14, None, ALU.mult), 12)
            nc.vector.tensor_scalar(half_gs[:, :], gs[:, :], 0.5, None, ALU.mult)
            nc.vector.scalar_tensor_tensor(c_ff[:, :], gs[:, :], bound[:, 3:4], us[:, :], ALU.mult, ALU.mult)
            step(nc.vector.tensor_scalar(ds_row[:, :], ds_row[:, :], bound[:, 2:3], None, ALU.mult), 13)

        @block.tensor
        def _(pe):
            def fill(n, part, signal):
                dst = pair_of_pieces(n)
                for k in range(2):
                    for i in range(4):
                        kc = 2 * (n % 2) + k
                        mm = nc.tensor.transpose(dst[:, k, i * P:(i + 1) * P],
                                                 part[:, n // 2, i, kc * P:(kc + 1) * P], ident[:, :])
                mm.then_inc(signal, 1)

            pe.wait_ge(ident_set, 1)
            for m in range(4):
                for n in range(4):
                    pe.wait_ge(w_hi_done if n < 2 else w_lo_done, m + 1)
                    wait(pe, wt_act if n % 2 == 0 else wt_dve, 2 * m + n // 2 - 1)
                    fill(n, w_part[m % 2], wt_mm)
            pe.wait_ge(wt_act, 8)
            pe.wait_ge(wt_dve, 8)

            def tile(t):
                for n in range(4):
                    pe.wait_ge(xhi_done if n < 2 else xlo_done, t + 1)
                    wait(pe, xt_act if n % 2 == 0 else xt_dve, 2 * t + n // 2 - 1)
                    fill(n, x_part, xt_mm)
                pe.wait_ge(xt_act, 2 * t + 2)
                pe.wait_ge(xt_dve, 2 * t + 2)
                for c in range(12):
                    wait(pe, lo_done, 12 * t + c - 3)
                    first = True
                    for wp, xp in TERMS:
                        for kc in range(KC):
                            if c < 8:
                                o = c % 4
                                lhs, rhs = w_t[c // 4][:, wp, kc, o * P:(o + 1) * P], x_t[:, xp, kc, :]
                            else:
                                i = c - 8
                                lhs, rhs = x_t[:, xp, kc, i * P:(i + 1) * P], w_t[2][:, wp, kc, :]
                            mm = nc.tensor.matmul(bank[2 + c % 4][:, :], lhs, rhs, start=first,
                                                  stop=((wp, xp) == TERMS[-1] and kc == KC - 1))
                            first = False
                    mm.then_inc(proj_mm, 1)

            over_tiles(pe, tile)


def attend(nc, x, out, q_dram, k_dram, v_dram, xn_dram, keep, bank):
    wo_t, wg8, wu8, wd8, ident, s_exp, c_out, half_gs, c_ff, ds_row = (
        keep[n] for n in ("wo_t", "wg8", "wu8", "wd8", "ident", "s_exp", "c_out", "half_gs", "c_ff", "ds_row"))
    x_v = x.rearrange("b (i p) d -> (b i) p d", p=P)
    out_v = out.rearrange("b (i p) d -> (b i) p d", p=P)
    with ExitStack() as ctx:
        def sb(name, shape, dt):
            return ctx.enter_context(nc.sbuf_tensor(name, shape, dt))

        def sem(name):
            return ctx.enter_context(nc.semaphore(name))

        q_st = [sb(f"q_st{i}", [3 * DK + 2, S], F16) for i in range(4)]
        k_st = [sb(f"k_st{i}", [3 * DK + 2, S], F16) for i in range(4)]
        v_sb = [sb(f"v_sb{i}", [P, QB, VE], F16) for i in range(4)]
        p32 = [sb(f"p32_{i}", [P, 512], F32) for i in range(RING)]
        probs = [sb(f"probs{i}", [P, 2, NE * 512], F16) for i in range(2)]
        mask = sb("mask", [P, 512], F32)
        junk = [sb(f"junk{i}", [P, 512], mybir.dt.bfloat16) for i in range(2)]
        mx = sb("mx", [P, 12], F32)
        m_part = sb("m_part", [P, 16], F16)
        m_row = [sb(f"m_row{i}", [16, P], F16) for i in range(2)]
        rsum = sb("rsum", [P, QB // 2], F32)
        o_low = sb("o_low", [P, QB // 2, DK], F32)
        o_sum = sb("o_sum", [P, QB // 2, DK], F32)
        attn = sb("attn", [P, 2, QB, D], F32)
        a_part = sb("a_part", [P, 2, D], F16)
        a_t = sb("a_t", [P, 2, KC, P], F16)
        xt = sb("xt", [P, 2, KC, FT], F16)
        th = [sb(f"th{i}", [P, FT], F32) for i in range(2)]
        ga = sb("ga", [P, FT], F32)
        fu = [sb(f"fu{i}", [P, FT], F32) for i in range(2)]
        fuse = sb("fuse", [P, 2, FC, FT], F16)
        ff_out = sb("ff_out", [P, D], F32)
        res = sb("res", [P, QB, D], F32)
        o_sb = [sb(f"o_sb{i}", [P, D], F32) for i in range(2)]

        st_bank, m_bank = bank[0:2], bank[2:4]
        o_bank, ff_bank, misc = bank[4], bank[5:7], bank[7]
        o_half = o_bank[:, 0:QB // 2 * VN].rearrange("p (i e) -> p i e", e=VN)

        q_loaded = [sem(f"q_loaded{i}") for i in range(4)]
        v_loaded = [sem(f"v_loaded{i}") for i in range(4)]
        row_loaded = [sem(f"row_loaded{i}") for i in range(4)]
        xt_loaded = sem("xt_loaded")
        xb_loaded = sem("xb_loaded")
        out_stored = [sem(f"out_stored{i}") for i in range(2)]
        ones_set = sem("ones_set2")
        mask_zero = sem("mask_zero")
        mask_set = sem("mask_set")
        m_mm = sem("m_mm")
        m_red = sem("m_red")
        m_link = sem("m_link")
        mt_mm = sem("mt_mm")
        mt_copied = sem("mt_copied")
        e_mm = sem("e_mm")
        exp_done = sem("exp_done")
        diag_done = sem("diag_done")
        p_hi = sem("p_hi")
        p_lo_dve = sem("p_lo_dve")
        p_lo_pool = sem("p_lo_pool")
        pv_mm = sem("pv_mm")
        o_link = sem("o_link")
        o_done = sem("o_done")
        ff_mm = sem("ff_mm")
        tanh_done = sem("tanh_done")
        ga_done = sem("ga_done")
        fu_done = sem("fu_done")
        fuse_hi = sem("fuse_hi")
        fuse_lo = sem("fuse_lo")
        down_mm = sem("down_mm")
        dn_link = sem("dn_link")
        res_done = sem("res_done")
        split_link = sem("split_link")
        split_done = sem("split_done")
        turn_mm = sem("turn_mm")
        turned = sem("turned")
        op_mm = sem("op_mm")
        o_ready = sem("o_ready")
        dve_waits = sem("dve_waits")
        pool_waits = sem("pool_waits")
        block = ctx.enter_context(nc.Block())

        def over_iterations(eng, step):
            step(0, False)
            with eng.Fori(1, LAG) as it:
                step(it, False)
            with eng.Fori(LAG, NIT) as it:
                step(it, True)

        def load_head(sp, n, i):
            for dst, dram, rows in ((q_st[i], q_dram, (HI, LO, HI)), (k_st[i], k_dram, (HI, HI, LO))):
                for r, w in enumerate(rows):
                    sp.dma_start(dst[r * DK:(r + 1) * DK, :], dram[w, ds(n, 1)].rearrange("a d t -> (a d) t")
                                 ).then_inc(q_loaded[i], 16)

        def load_v(sp, n, i):
            sp.dma_start(v_sb[i][:, :, :], v_dram[ds(n, 1)].rearrange("a p k e -> p (a k) e")
                         ).then_inc(v_loaded[i], 16)

        def take_low(eng, ops, units, it, k, signal):
            if k % NE not in units or (isinstance(it, int) and it == 0 and k < 0):
                return
            s, u = k // NE, k % NE
            at = slice(u * 512, (u + 1) * 512)
            eng.wait_ge(p_hi, STEPS * it + k + 1)
            ops.tensor_tensor(probs[s % 2][:, LO, at], p32[k % RING][:, :], probs[s % 2][:, HI, at],
                              ALU.subtract).then_inc(signal, 1)

        @block.sync
        def _(sp):
            def load_tile(t):
                sp.dma_start(xt[:, :, :, :].rearrange("p w k t -> p (w k) t"),
                             xn_dram[ds(t, 1)].rearrange("a p w k t -> p (a w k) t")).then_inc(xt_loaded, 16)

            def store_row(i, m):
                sp.wait_ge(mt_copied, m)
                sp.dma_start(q_st[i][3 * DK:3 * DK + 2, :], m_row[i % 2][:, :]).then_inc(row_loaded[i], 16)

            for n in range(3):
                load_head(sp, n, n)
                if n < 2:
                    load_v(sp, n, n)
            load_tile(0)
            store_row(0, 1)

            def iteration(it, with_out):
                for s in range(HEADS_PER_IT):
                    n = 4 * it + s
                    wait(sp, e_mm, NE * n)
                    load_head(sp, (n + 3) % NH, (s + 3) % 4)
                    wait(sp, pv_mm, 2 * (n - 1))
                    load_v(sp, (n + 2) % NH, (s + 2) % 4)
                    if with_out and s in (1, 2):
                        store_out(2 * (it - LAG) + s - 1, s - 1, it - LAG)
                    if s == 2:
                        sp.dma_start(res[:, ds(it % 4 * 2, 2), :],
                                     x_v[ds(2 * it, 2)].rearrange("a p d -> p a d")).then_inc(xb_loaded, 16)
                    if s == 3:
                        sp.wait_ge(ff_mm, FC * (it + 1))
                        load_tile((it + 1) % NIT)
                    store_row((s + 1) % 4, n + 2)

            def store_out(b, i, r):
                sp.wait_ge(o_ready, 2 * r + i + 1)
                sp.dma_start(out_v[ds(b, 1)].rearrange("a p d -> p (a d)"), o_sb[i][:, :]).then_inc(out_stored[i], 16)

            over_iterations(sp, iteration)
            with sp.Fori(NIT, NIT + LAG) as it:
                for i in range(2):
                    store_out(2 * (it - LAG) + i, i, it - LAG)
            for i in range(2):
                sp.wait_ge(out_stored[i], 16 * NIT)
                sp.wait_ge(row_loaded[i], 16 * (NIT + (i == 0)))
            for i in range(4):
                sp.wait_ge(q_loaded[i], 96 * (NIT + (i < 3)))
                sp.wait_ge(v_loaded[i], 16 * (NIT + (i < 2)))
            sp.wait_ge(xt_loaded, 16 * (NIT + 1))

        @block.gpsimd
        def _(pool):
            nc.gpsimd.memset(mask[:, :], 0.0).then_inc(mask_zero, 1)
            pool.wait_ge(mask_zero, 1)
            nc.gpsimd.affine_select(out=mask[:, 512 - P:512], in_=mask[:, 512 - P:512], compare_op=ALU.is_ge,
                                    fill=MASKED, base=0, pattern=[[-1, P]], channel_multiplier=1
                                    ).then_inc(mask_set, 1)

            def low_of_fuse(g, f, it):
                pool.wait_ge(fuse_hi, g + 1)
                nc.gpsimd.tensor_tensor(fuse[:, LO, f, :], fu[f % 2][:, :], fuse[:, HI, f, :],
                                        ALU.subtract).then_inc(fuse_lo, 1)

            def iteration(it, with_out):
                for s in range(HEADS_PER_IT):
                    for u in range(NE):
                        if u in DIAGONAL:
                            wait_apart(pool, exp_done, NE * (4 * it + s) + u + 1, pool_waits)
                            blocks = 2 if DIAGONAL[u] else 1
                            step = DIAGONAL[u] or P
                            at = p32[(s * NE + u) % RING][:, :].rearrange("p (b q) -> p b q", q=P)
                            at = at[:, 0:(blocks - 1) * (step // P) + 1:step // P, :]
                            nc.gpsimd.affine_select(out=at, in_=at, compare_op=ALU.is_ge, fill=0.0, base=0,
                                                    pattern=[[0, blocks], [1, P]], channel_multiplier=-1
                                                    ).then_inc(diag_done, 1)
                        take_low(pool, nc.gpsimd, POOL_LOW, it, s * NE + u - 2, p_lo_pool)
                        if s * NE + u - 3 in FFN_STEP:
                            f = FFN_STEP[s * NE + u - 3]
                            low_of_fuse(FC * it + f, f, it)

            over_iterations(pool, iteration)
            for k in (STEPS - 2, STEPS - 1):
                take_low(pool, nc.gpsimd, POOL_LOW, NIT - 1, k, p_lo_pool)

        @block.scalar
        def _(act):
            def take_high(it, k):
                if isinstance(it, int) and it == 0 and k < 0:
                    return
                s, u = k // NE, k % NE
                act.wait_ge(exp_done, STEPS * it + k + 1)
                if u in DIAGONAL:
                    act.wait_ge(diag_done, ND * (HEADS_PER_IT * it + s) + sorted(DIAGONAL).index(u) + 1)
                if u == 0:
                    wait(act, pv_mm, 2 * (HEADS_PER_IT * it + s - 1))
                nc.scalar.copy(probs[s % 2][:, HI, u * 512:(u + 1) * 512], p32[k % RING][:, :]).then_inc(p_hi, 1)

            def iteration(it, with_out):
                for s in range(HEADS_PER_IT):
                    n = HEADS_PER_IT * it + s
                    for u in range(NE):
                        k = s * NE + u
                        e = NE * n + u
                        act.wait_ge(e_mm, e + 1)
                        old = k - RING
                        if old % NE in POOL_LOW:
                            wait(act, p_lo_pool, HEADS_PER_IT * len(POOL_LOW) * it + low_parts(POOL_LOW, old))
                        else:
                            wait(act, p_lo_dve, HEADS_PER_IT * len(DVE_LOW) * it + low_parts(DVE_LOW, old))
                        nc.scalar.activation(p32[k % RING][:, :], st_bank[(s + u) % 2][:, :],
                                             ACT.Exp, scale=s_exp[:, :]).then_inc(exp_done, 1)
                        take_high(it, k - 1)
                        if k - 1 in FFN_STEP:
                            f = FFN_STEP[k - 1]
                            g = FC * it + f
                            act.wait_ge(ff_mm, g + 1)
                            wait(act, ga_done, g - 1)
                            nc.scalar.activation(th[f % 2][:, :], ff_bank[f % 2][:, 0:FT], ACT.Tanh,
                                                 scale=half_gs[:, f:f + 1]).then_inc(tanh_done, 1)
                        if k - 3 in FFN_STEP:
                            f = FFN_STEP[k - 3]
                            g = FC * it + f
                            act.wait_ge(fu_done, g + 1)
                            if f == 0:
                                wait(act, down_mm, 2 * it)
                            nc.scalar.copy(fuse[:, HI, f, :], fu[f % 2][:, :]).then_inc(fuse_hi, 1)

            over_iterations(act, iteration)
            take_high(NIT - 1, STEPS - 1)

        @block.vector
        def _(dve):
            def row_maxima(m, units):
                for u in units:
                    i, k0, w, col = M_UNITS[u]
                    if u == 0 and not (isinstance(m, int) and m == 0):
                        wait_apart(dve, m_link, 3 * m, dve_waits)
                    if k0 + w == (i + 1) * P:
                        wait_apart(dve, m_mm, NM * m + u + 1, dve_waits)
                    else:
                        dve.wait_ge(m_mm, NM * m + u + 1)
                    src = m_bank[u % 2][:, 0:w]
                    if k0 + w == (i + 1) * P:
                        ins = nc.vector.tensor_tensor_reduce(
                            out=junk[u % 2][:, 0:w], in0=src, in1=mask[:, 512 - w:512], scale=1.0, scalar=MASKED,
                            op0=ALU.add, op1=ALU.max, accum_out=mx[:, col:col + 1])
                    else:
                        ins = nc.vector.tensor_reduce(mx[:, col:col + 1], src, AX.X, ALU.max)
                    ins.then_inc(m_red, 1)

            def split_maxima(m):
                dve.wait_ge(m_red, NM * (m + 1))
                nc.vector.tensor_tensor(mx[:, 4:8], mx[:, 4:8], mx[:, 8:12], ALU.max).then_inc(m_link, 1)
                dve.wait_ge(m_link, 3 * m + 1)
                wait(dve, mt_mm, m)
                nc.vector.tensor_scalar(m_part[:, 0:8], mx[:, 0:8], -1.0 / MSCALE, None, ALU.mult
                                        ).then_inc(m_link, 1)
                dve.wait_ge(m_link, 3 * m + 2)
                nc.vector.scalar_tensor_tensor(m_part[:, 8:16], mx[:, 0:8], -1.0 / MSCALE, m_part[:, 0:8],
                                               ALU.mult, ALU.subtract).then_inc(m_link, 1)

            def copy_row(m, i, last_use):
                dve.wait_ge(mt_mm, m + 1)
                wait(dve, row_loaded[(i + 2) % 4], 16 * last_use)
                nc.vector.tensor_copy(m_row[i % 2][:, :], misc[0:16, 0:P // 2].bitcast(F16)
                                      ).then_inc(mt_copied, 1)

            def normalise(n, half):
                batch, head = n // H, n % H
                dve.wait_ge(pv_mm, 2 * n + half + 1)
                nc.vector.tensor_copy(o_low[:, :, :], o_half[:, :, 0:DK])
                nc.vector.reciprocal(rsum[:, :], o_half[:, :, 2 * DK]).then_inc(o_link, 1)
                dve.wait_ge(o_link, 4 * n + 2 * half + 1)
                nc.vector.tensor_tensor(o_sum[:, :, :], o_half[:, :, DK:2 * DK], o_low[:, :, :],
                                        ALU.add).then_inc(o_link, 1)
                dve.wait_ge(o_link, 4 * n + 2 * half + 2)
                blocks = slice(half * QB // 2, (half + 1) * QB // 2)
                dst = attn[:, ds(batch % 2, 1), blocks, ds(head * DK, DK)].rearrange("p a i d -> p (a i) d")
                nc.vector.tensor_tensor(dst, o_sum[:, :, :],
                                        rsum[:, :].unsqueeze(2).broadcast_to([P, QB // 2, DK]),
                                        ALU.mult).then_inc(o_done, 1)

            def split_attention(i, r):
                par, blk = (r // 4) % 2, (r % 4) * 2 + i
                src = attn[:, ds(par, 1), ds(blk, 1), :].rearrange("p a i d -> p (a i d)")
                wait(dve, turn_mm, 2 * r + i)
                nc.vector.tensor_copy(a_part[:, HI, :], src).then_inc(split_link, 1)
                dve.wait_ge(split_link, 2 * r + i + 1)
                nc.vector.tensor_tensor(a_part[:, LO, :], src, a_part[:, HI, :], ALU.subtract
                                        ).then_inc(split_done, 1)

            def copy_turned(i, r):
                dve.wait_ge(turn_mm, 2 * r + i + 1)
                nc.vector.tensor_copy(a_t[:, :, :, :].rearrange("p w k t -> p (w k t)"),
                                      misc[:, :].bitcast(F16)).then_inc(turned, 1)

            def add_output(i, r):
                dve.wait_ge(op_mm, 2 * r + i + 1)
                wait(dve, out_stored[i], 16 * r)
                blk = (r % 4) * 2 + i
                nc.vector.scalar_tensor_tensor(
                    o_sb[i][:, :], misc[:, :], c_out[:, 0:1],
                    res[:, ds(blk, 1), :].rearrange("p a d -> p (a d)"), ALU.mult, ALU.add).then_inc(o_ready, 1)

            def add_down(i, it):
                at = res[:, ds(it % 4 * 2 + i, 1), :].rearrange("p a d -> p (a d)")
                dve.wait_ge(down_mm, 2 * it + i + 1)
                nc.vector.tensor_tensor(ff_out[:, :], misc[:, :], ds_row[:, :], ALU.mult).then_inc(dn_link, 1)
                dve.wait_ge(dn_link, 2 * it + i + 1)
                dve.wait_ge(xb_loaded, 16 * (it + 1))
                nc.vector.tensor_tensor(at, ff_out[:, :], at, ALU.add).then_inc(res_done, 1)

            for i in range(4):
                last = nc.vector.memset(k_st[i][3 * DK:3 * DK + 2, :], MSCALE)
            last.then_inc(ones_set, 1)
            dve.wait_ge(mask_set, 1)
            row_maxima(0, range(NM))
            split_maxima(0)
            copy_row(0, 0, 0)
            row_maxima(1, range(NM))

            def iteration(it, with_out):
                for s in range(HEADS_PER_IT):
                    n = 4 * it + s
                    for u in range(NE):
                        k = s * NE + u
                        if u == 0:
                            split_maxima(n + 1)
                        if k - 2 in FFN_STEP:
                            f = FFN_STEP[k - 2]
                            g = FC * it + f
                            dve.wait_ge(tanh_done, g + 1)
                            wait(dve, fu_done, g)
                            nc.vector.scalar_tensor_tensor(ga[:, :], th[f % 2][:, :], 1.0, ff_bank[f % 2][:, 0:FT],
                                                           ALU.add, ALU.mult).then_inc(ga_done, 1)
                            dve.wait_ge(ga_done, g + 1)
                            wait(dve, fuse_lo, g - 1)
                            nc.vector.scalar_tensor_tensor(fu[f % 2][:, :], ff_bank[f % 2][:, FT:2 * FT],
                                                           c_ff[:, f:f + 1], ga[:, :], ALU.mult, ALU.mult
                                                           ).then_inc(fu_done, 1)
                        row_maxima(n + 2, M_STEP.get(u, ()))
                        take_low(dve, nc.vector, DVE_LOW, it, k - 2, p_lo_dve)
                        if u == ROW_STEP:
                            copy_row(n + 1, (s + 1) % 4, it if s == 0 else it + 1)
                        if u in (3, NE - 1) and not (isinstance(it, int) and n == 0):
                            normalise(n - 1, int(u == NE - 1))
                        if with_out:
                            if k in SPLIT_STEP:
                                split_attention(SPLIT_STEP[k], it - LAG)
                            if k in TURN_STEP:
                                copy_turned(TURN_STEP[k], it - LAG)
                            if k in ADD_OUT_STEP:
                                add_output(ADD_OUT_STEP[k], it - LAG)
                        if k in ADD_DOWN_STEP and not isinstance(it, int):
                            add_down(ADD_DOWN_STEP[k], it - 1)

            over_iterations(dve, iteration)
            for k in (STEPS - 2, STEPS - 1):
                take_low(dve, nc.vector, DVE_LOW, NIT - 1, k, p_lo_dve)
            for half in range(2):
                normalise(NH - 1, half)
            dve.wait_ge(o_done, 2 * NH)
            for i in range(2):
                add_down(i, NIT - 1)
            with dve.Fori(NIT, NIT + LAG) as it:
                for i in range(2):
                    split_attention(i, it - LAG)
                    copy_turned(i, it - LAG)
                    add_output(i, it - LAG)

        @block.tensor
        def _(pe):
            def maxima_scores(m, i, units):
                rows = slice(0, 3 * DK)
                for u in units:
                    blk, k0, w, _ = M_UNITS[u]
                    wait(pe, m_red, NM * m + u - 1)
                    nc.tensor.matmul(m_bank[u % 2][:, 0:w], q_st[i][rows, blk * P:(blk + 1) * P],
                                     k_st[i][rows, k0:k0 + w], start=True, stop=True).then_inc(m_mm, 1)

            def turn_maxima(m):
                pe.wait_ge(m_link, 3 * (m + 1))
                nc.tensor.transpose(misc[0:16, 0:P // 2].bitcast(F16), m_part[:, :], ident[:, :]
                                    ).then_inc(mt_mm, 1)

            def scores(n, s, u):
                e = NE * n + u
                wait(pe, exp_done, e - 1)
                at = 0
                for j, q0, w in E_UNITS[u]:
                    mm = nc.tensor.matmul(st_bank[(s + u) % 2][:, at:at + w], k_st[s][:, j * P:(j + 1) * P],
                                          q_st[s][:, q0:q0 + w], start=True, stop=True)
                    at += w
                mm.then_inc(e_mm, 1)

            def values(n, s, i):
                if i % (QB // 2) == 0:
                    wait(pe, o_done, 2 * n + i // (QB // 2))
                for j in range(i + 1):
                    at = p_column(j, i)
                    for part in (HI, LO):
                        mm = nc.tensor.matmul(o_half[:, i % (QB // 2), :], probs[s % 2][:, part, at:at + P],
                                              v_sb[s][:, j, 0:VN], start=(j == 0 and part == HI),
                                              stop=(j == i and part == LO))
                if i % (QB // 2) == QB // 2 - 1:
                    mm.then_inc(pv_mm, 1)

            def start_values(n, s, uses, units):
                if units < NE:
                    pe.wait_ge(v_loaded[s], 16 * uses)
                pe.wait_ge(p_lo_dve, len(DVE_LOW) * n + low_parts(DVE_LOW, units - 1))
                pe.wait_ge(p_lo_pool, len(POOL_LOW) * n + low_parts(POOL_LOW, units - 1))

            def feed_forward(g, f, it):
                if f == 0:
                    pe.wait_ge(xt_loaded, 16 * (it + 1))
                wait(pe, fu_done, g - 1)
                for h, w8 in enumerate((wg8, wu8)):
                    for part in (HI, LO):
                        for kc in range(KC):
                            mm = nc.tensor.matmul(ff_bank[f % 2][:, h * FT:(h + 1) * FT],
                                                  w8[:, kc, f * P:(f + 1) * P], xt[:, part, kc, :],
                                                  start=(part == HI and kc == 0), stop=(part == LO and kc == KC - 1))
                mm.then_inc(ff_mm, 1)

            def down(i, half, it):
                if half == 0:
                    pe.wait_ge(fuse_lo, FC * (it + 1))
                    pe.wait_ge(*((res_done, 2 * it + 1) if i else (mt_copied, 4 * it + 5)))
                for f in range(half * FC // 2, (half + 1) * FC // 2):
                    for part in (HI, LO):
                        mm = nc.tensor.matmul(misc[:, :], fuse[:, part, f, i * P:(i + 1) * P], wd8[:, f, :],
                                              start=(f == 0 and part == HI), stop=(f == FC - 1 and part == LO))
                if half == 1:
                    mm.then_inc(down_mm, 1)

            def turn_attention(i, r):
                pe.wait_ge(split_done, 2 * r + i + 1)
                dst = misc[:, :].bitcast(F16).rearrange("p (w k t) -> p w k t", w=2, k=KC)
                for part in (HI, LO):
                    for kc in range(KC):
                        mm = nc.tensor.transpose(dst[:, part, kc, :], a_part[:, part, kc * P:(kc + 1) * P],
                                                 ident[:, :])
                mm.then_inc(turn_mm, 1)

            def project(i, half, r):
                if half == 0:
                    pe.wait_ge(turned, 2 * r + i + 1)
                products = [(ap, wp, kc) for ap, wp in TERMS for kc in range(KC)]
                for m, (ap, wp, kc) in list(enumerate(products))[half * 6:half * 6 + 6]:
                    mm = nc.tensor.matmul(misc[:, :], a_t[:, ap, kc, :], wo_t[:, wp, kc, :],
                                          start=(m == 0), stop=(m == len(products) - 1))
                if half == 1:
                    mm.then_inc(op_mm, 1)

            pe.wait_ge(ones_set, 1)
            pe.wait_ge(q_loaded[0], 96)
            maxima_scores(0, 0, range(NM))
            turn_maxima(0)
            pe.wait_ge(q_loaded[1], 96)
            maxima_scores(1, 1, range(NM))

            def iteration(it, with_out):
                first = isinstance(it, int)
                r = it - LAG
                for s in range(HEADS_PER_IT):
                    n = 4 * it + s
                    for u in range(NE):
                        k = s * NE + u
                        if u == 0:
                            pe.wait_ge(row_loaded[s], 16 * (it + 1))
                        scores(n, s, u)
                        if u == 1:
                            pe.wait_ge(q_loaded[(s + 2) % 4], 96 * ((it + 1) if s < 2 else (it + 2)))
                        maxima_scores(n + 2, (s + 2) % 4, M_STEP.get(u, ()))
                        if not (first and n == 0):
                            if u in (1, 5):
                                start_values(n - 1, (s + 3) % 4, it if s == 0 else it + 1, 3 if u == 1 else NE)
                            for i in PV_STEP.get(u, ()):
                                values(n - 1, (s + 3) % 4, i)
                        if u == ROW_STEP:
                            if s == 0 and not first:
                                pe.wait_ge(res_done, 2 * it)
                            elif s in (1, 2) and with_out:
                                pe.wait_ge(o_ready, 2 * r + s)
                            else:
                                pe.wait_ge(mt_copied, n + 1)
                            turn_maxima(n + 1)
                        if k in FFN_STEP:
                            feed_forward(FC * it + FFN_STEP[k], FFN_STEP[k], it)
                        if with_out:
                            if k in TURN_STEP:
                                pe.wait_ge(mt_copied, 4 * it + 2 + TURN_STEP[k])
                                turn_attention(TURN_STEP[k], r)
                            if k in PROJ_STEP:
                                project(*PROJ_STEP[k], r)
                        if k in DOWN_STEP and not first:
                            down(*DOWN_STEP[k], it - 1)

            over_iterations(pe, iteration)
            start_values(NH - 1, 3, NIT, 3)
            start_values(NH - 1, 3, NIT, NE)
            for i in range(QB):
                values(NH - 1, 3, i)
            for step in DOWN_STEP.values():
                down(*step, NIT - 1)
            pe.wait_ge(res_done, 2 * NIT)
            with pe.Fori(NIT, NIT + LAG) as it:
                for i in range(2):
                    pe.wait_ge(o_ready, 2 * (it - LAG) + i)
                    turn_attention(i, it - LAG)
                    for half in range(2):
                        project(i, half, it - LAG)


def build(nc, x, wq, wk, wv, wo, gate_w, up_w, down_w, gate_s, up_s, down_s, out):
    q_dram = nc.dram_tensor("q_parts", (2, NH, DK, S), F16, kind="Internal").ap()
    k_dram = nc.dram_tensor("k_parts", (2, NH, DK, S), F16, kind="Internal").ap()
    v_dram = nc.dram_tensor("v_parts", (NH, P, QB, VE), F16, kind="Internal").ap()
    xn_dram = nc.dram_tensor("xn_parts", (NIT, P, 2, KC, FT), F16, kind="Internal").ap()
    with ExitStack() as ctx:
        def sb(name, shape, dt):
            return ctx.enter_context(nc.sbuf_tensor(name, shape, dt))

        bank = [ctx.enter_context(nc.psum_tensor(f"bank{i}", [P, 512], F32)) for i in range(8)]
        keep = {"wo_t": sb("wo_t", [P, 2, KC, D], F16), "wg8": sb("wg8", [P, KC, INNER], F16),
                "wu8": sb("wu8", [P, KC, INNER], F16), "wd8": sb("wd8", [P, FC, D], F16),
                "ident": sb("ident", [P, P], F16), "s_exp": sb("s_exp", [P, 1], F32),
                "c_out": sb("c_out", [P, 1], F32), "half_gs": sb("half_gs", [P, FC], F32),
                "c_ff": sb("c_ff", [P, FC], F32), "ds_row": sb("ds_row", [P, D], F32)}
        prepare(nc, x, (wq, wk, wv, wo), (gate_w, up_w, down_w), (gate_s, up_s, down_s),
                q_dram, k_dram, v_dram, xn_dram, keep, bank)
        attend(nc, x, out, q_dram, k_dram, v_dram, xn_dram, keep, bank)


_INS = ["L0_attn_x", "L0_attn_Wq", "L0_attn_Wk", "L0_attn_Wv", "L0_attn_Wo", "L0_ffn_gate_w", "L0_ffn_up_w",
        "L0_ffn_down_w", "L0_ffn_gate_scale", "L0_ffn_up_scale", "L0_ffn_down_scale"]


def kernel(**inputs):
    import numpy as _np
    import concourse.bacc as _bacc
    from concourse import mybir as _mybir
    from concourse.bass_utils import run_bass_kernel_spmd as _run

    nc = _bacc.Bacc("TRN2", target_bir_lowering=False, num_devices=1)
    arrays, args = {}, []
    for name in _INS:
        a = _np.ascontiguousarray(inputs[name])
        arrays[f"in_{name}"] = a
        args.append(nc.dram_tensor(f"in_{name}", a.shape, _mybir.dt.from_np(a.dtype), kind="ExternalInput").ap())
    args.append(nc.dram_tensor("out_0", (B, S, D), F32, kind="ExternalOutput").ap())
    build(nc, *args)
    r = _run(nc, [arrays], core_ids=[0])
    return r.results[0]["out_0"]
```

```python
from contextlib import ExitStack

import concourse.bass as bass
from concourse import mybir

F32 = mybir.dt.float32
F16 = mybir.dt.float16
I32 = mybir.dt.int32
U32 = mybir.dt.uint32
ALU = mybir.AluOpType
ACT = mybir.ActivationFunctionType
AX = mybir.AxisListType
RMAX = bass.bass_isa.ReduceOp.max
ds = bass.ds

P = 128
B, S, D = 4, 1024, 512
H, DK = 16, 32
INNER = 1536
KC = D // P
FC = INNER // P
NH = B * H
TILE = 512
NT = B * S // TILE
NB = TILE // P
QB = S // P
VE = 2 * DK + 2
VN = 2 * DK + 1
HI, LO = 0, 1
TERMS = ((HI, HI), (HI, LO), (LO, HI))
EPS = 1e-5
NEWTON = 3
GUESS = float(0x5F3759DF)
EXP_BITS = 0x7F800000
MSCALE = 1024.0
MASKED = -3.0e38

HEADS_PER_IT = 4
NIT = NH // HEADS_PER_IT
LAG = S // (2 * P)
FT = 2 * P

WEIGHTS_SPLIT = {(0, 2): (2,), (1, 3): (3,)}
WEIGHTS_COPIED = {(0, 3): (1,), (0, 5): (2,), (1, 8): (3,)}
X_TURNED = 10

M_UNITS = ([(i, 0, (i + 1) * P, i) for i in range(4)]
           + [u for i in range(4, 8) for u in ((i, 0, 512, i), (i, 512, (i + 1) * P - 512, i + 4))])
E_UNITS = [[(0, 0, 512)], [(1, 128, 384), (3, 384, 128)], [(2, 256, 256), (6, 768, 256)],
           [(0, 512, 512)], [(1, 512, 512)], [(2, 512, 512)], [(3, 512, 512)],
           [(4, 512, 512)], [(5, 640, 384), (7, 896, 128)]]
NM, NE = len(M_UNITS), len(E_UNITS)
DIAGONAL = {0: 0, 1: 384, 2: 256, 7: 0, 8: 384}
ND = len(DIAGONAL)


def p_column(j, i):
    for u, pieces in enumerate(E_UNITS):
        at = u * 512
        for key, q0, w in pieces:
            if key == j and q0 <= i * P < q0 + w:
                return at + i * P - q0
            at += w


POOL_LOW = (1, 2, 3, 4, 5, 6, 7)
DVE_LOW = tuple(u for u in range(NE) if u not in POOL_LOW)
RING = 6
FU = 3
STEPS = HEADS_PER_IT * NE


def low_parts(units, k):
    return len(units) * (k // NE) + sum(u <= k % NE for u in units)


M_STEP = {1: (0, 1), 2: (2,), 3: (3,), 4: (4,), 5: (5, 6), 6: (7, 8), 7: (9, 10), 8: (11,)}
PV_STEP = {1: (0, 1), 2: (2,), 3: (3,), 5: (4,), 6: (5,), 7: (6,), 8: (7,)}
ROW_STEP = {6: 0, 15: 1, 23: 2, 32: 3}
DOWN_STEP = {0: [(0, 0), (0, 1)], 1: [(0, 2)], 2: [(0, 3)], 3: [(0, 4)], 4: [(0, 5)],
             9: [(1, 0), (1, 1)], 10: [(1, 2)], 11: [(1, 3)], 12: [(1, 4)], 13: [(1, 5)]}
DOWN_PIECES = 6
ADD_DOWN_STEP = {5: 0, 14: 1}
GATE_STEP = {4: 0, 6: 1, 8: 2, 14: 3, 16: 4, 18: 5, 22: 6, 23: 7, 25: 8, 27: 9, 31: 10, 33: 11}
UP_STEP = {5: 0, 7: 1, 13: 2, 15: 3, 17: 4, 18: 5, 22: 6, 24: 7, 26: 8, 27: 9, 31: 10, 34: 11}
TANH_STEP = {k + 1: f for k, f in UP_STEP.items()}
SWIGLU_STEP = {k + 2: f for k, f in UP_STEP.items()}
FUSE_STEP = {**{k + 3: f for k, f in UP_STEP.items() if f > 1}, 14: 0, 15: 1}
SPLIT_STEP = {13: 0, 21: 1}
TURN_STEP = {17: 0, 25: 1}
PROJ_STEP = {19: [(0, 0)], 20: [(0, 1)], 21: [(0, 2)], 28: [(1, 0)], 29: [(1, 1)], 30: [(1, 2)]}
PROJ_PIECES = 3
ADD_OUT_STEP = {22: 0, 31: 1}


def at_step(table, it, k):
    found = [(table[k], it)] if k in table else []
    if k + STEPS in table and not isinstance(it, int):
        found.append((table[k + STEPS], it - 1))
    return found


def wait(eng, sem, value):
    if isinstance(value, int) and value <= 0:
        return
    eng.wait_ge(sem, value)


def wait_apart(eng, sem, value, counted):
    eng.wait_ge(sem, value)
    if not isinstance(value, int):
        eng.sem_inc(counted, 1)


def prepare(nc, x, weights, ffn, scales, q_dram, k_dram, v_dram, xn_dram, keep, bank):
    wo_t, wg8, wu8, wd8, ident, s_exp, c_out, half_gs, c_ff, ds_row = (
        keep[n] for n in ("wo_t", "wg8", "wu8", "wd8", "ident", "s_exp", "c_out", "half_gs", "c_ff", "ds_row"))
    gate_w, up_w, down_w = ffn
    x_v = x.rearrange("b (u k p) d -> (b u) p k d", k=NB, p=P)
    GC = INNER // 2
    DCOL = D // NT
    gate_v = gate_w.rearrange("(k p) (h f) -> k h p f", p=P, h=2)
    up_v = up_w.rearrange("(k p) (h f) -> k h p f", p=P, h=2)
    down_v = down_w.rearrange("(c p) (t o) -> t p c o", p=P, o=DCOL)
    with ExitStack() as ctx:
        def sb(name, shape, dt):
            return ctx.enter_context(nc.sbuf_tensor(name, shape, dt))

        def sem(name):
            return ctx.enter_context(nc.semaphore(name))

        w_raw = [sb(f"w_raw{m}", [P, KC, D], F32) for m in range(4)]
        w_part = [sb(f"w_part{i}", [P, 2, KC, D], F16) for i in range(2)]
        w_t = [sb(f"w_t{m}", [P, 2, KC, D], F16) for m in range(3)] + [wo_t]
        w_max = sb("w_max", [P, 4], F32)
        w_gmax = sb("w_gmax", [P, 4], F32)
        w_pow = sb("w_pow", [P, 4], F32)
        w_inv = sb("w_inv", [P, 4], F32)
        x_in = sb("x_in", [P, NB, D], F32)
        xn = sb("xn", [P, NB, D], F32)
        x_part = sb("x_part", [P, 2, NB, D], F16)
        x_t = [sb(f"x_t{i}", [P, 2, KC, TILE], F16) for i in range(2)]
        stats = sb("stats", [P, NB, 6], F32)
        mv = sb("mv", [P, NB, 2], F32)
        var = sb("var", [P, NB], F32)
        rstd = sb("rstd", [P, NB], F32)
        nt0 = sb("nt0", [P, NB], F32)
        nt1 = sb("nt1", [P, NB], F32)
        qk_st = [sb(f"qk_st{i}", [P, 2, TILE], F16) for i in range(4)]
        v_st = sb("v_st", [P, H, NB, VE], F16)
        raw = sb("raw", [P, 3, GC], F32)
        cmag = sb("cmag", [P, 3, GC], F32)
        ff_max = sb("ff_max", [P, 2, NT], F32)
        ff4 = sb("ff4", [P, 4], F32)
        ff4g = sb("ff4g", [P, 4], F32)
        bound = sb("bound", [P, 4], F32)
        gs = sb("gs", [P, FC], F32)
        us = sb("us", [P, FC], F32)

        w_loaded = [sem(f"w_loaded{m}") for m in range(4)]
        small_loaded = sem("small_loaded")
        x_loaded = sem("x_loaded")
        ffw_loaded = sem("ffw_loaded")
        ident_set = sem("ident_set")
        ident_zero = sem("ident_zero")
        ones_set = sem("ones_set")
        wmax_done = sem("wmax_done")
        pow_link = sem("pow_link")
        wgmax_done = sem("wgmax_done")
        winv_done = sem("winv_done")
        w_hi_done = sem("w_hi_done")
        w_lo_done = sem("w_lo_done")
        wt_mm = sem("wt_mm")
        wt_act = sem("wt_act")
        wt_dve = sem("wt_dve")
        ln_link = sem("ln_link")
        xn_done = sem("xn_done")
        xhi_done = sem("xhi_done")
        xlo_done = sem("xlo_done")
        xt_mm = sem("xt_mm")
        xt_act = sem("xt_act")
        xt_dve = sem("xt_dve")
        proj_mm = sem("proj_mm")
        hi_done = sem("hi_done")
        lo_done = sem("lo_done")
        qk_stored = [sem(f"qk_stored{i}") for i in range(4)]
        v_stored = sem("v_stored")
        xt_stored = sem("xt_stored")
        round_link = sem("round_link")
        rounded = sem("rounded")
        ffmax_done = sem("ffmax_done")
        ffg_done = sem("ffg_done")
        fin_link = sem("fin_link")
        waits_apart = sem("waits_apart")
        block = ctx.enter_context(nc.Block())
        LINKS = 4 + 4 * NEWTON
        ROUND_LINKS = 3

        def over_tiles(eng, tile):
            tile(0, 0)
            tile(1, 1)
            with eng.Fori(1, NT // 2 - 1) as pair:
                for i in range(2):
                    tile(2 * pair + i, i)
            for i in range(2):
                tile(NT - 2 + i, i)

        def has_next(t):
            return not (isinstance(t, int) and t == NT - 1)

        @block.sync
        def _(sp):
            def load_ffn_weights(t):
                for i, src in enumerate((gate_v, up_v)):
                    sp.dma_start(raw[:, i:i + 1, :],
                                 src[ds(t // 2, 1), ds(t % 2, 1)].rearrange("k h p f -> p (k h) f")
                                 ).then_inc(ffw_loaded, 16)
                sp.dma_start(raw[:, 2, :].rearrange("p (c o) -> p c o", c=FC),
                             down_v[ds(t, 1)].rearrange("a p c o -> p (a c) o")).then_inc(ffw_loaded, 16)

            def load_x(t):
                wait(sp, xn_done, t)
                sp.dma_start(x_in[:, :, :], x_v[ds(t, 1)].rearrange("a p k d -> p (a k) d")).then_inc(x_loaded, 16)

            for m, w in enumerate(weights):
                sp.dma_start(w_raw[m][:, :, :], w.rearrange("(c p) k -> p c k", p=P)).then_inc(w_loaded[m], 16)
                if m in (0, 2):
                    load_x(m // 2)
            load_ffn_weights(0)
            gate_s, up_s, down_s = scales
            with nc.allow_non_contiguous_dma(reason="two vectors of 1536 scales"):
                sp.dma_start(gs[:, :], gate_s.rearrange("(c p) -> p c", p=P)).then_inc(small_loaded, 16)
                sp.dma_start(us[:, :], up_s.rearrange("(c p) -> p c", p=P)).then_inc(small_loaded, 16)
            sp.dma_start(ds_row[:, :], down_s.rearrange("(a d) -> a d", a=1).broadcast_to([P, D])).then_inc(
                small_loaded, 16)

            def tile(t, par):
                sp.wait_ge(xt_act, 2 * t + 2)
                sp.wait_ge(xt_dve, 2 * t + 2)
                for half in range(2):
                    sp.dma_start(xn_dram[ds(2 * t + half, 1)].rearrange("a p w k t -> p (a w k) t"),
                                 x_t[par][:, :, :, half * FT:(half + 1) * FT].rearrange("p w k t -> p (w k) t")
                                 ).then_inc(xt_stored, 16)
                for c in range(8):
                    dst = (q_dram if c < 4 else k_dram).rearrange(
                        "w (b c a) d (u t) -> b u c (a d) w t", b=B, c=KC, u=2)
                    sp.wait_ge(lo_done, 12 * t + c + 1)
                    sp.dma_start(dst[ds(t // 2, 1), ds(t % 2, 1), c % 4].rearrange("b u p w t -> p (b u w) t"),
                                 qk_st[c % 4][:, :, :]).then_inc(qk_stored[c % 4], 16)
                    if c == (6 if isinstance(t, int) and t == 0 else 3) and not (isinstance(t, int) and t >= NT - 2):
                        load_x(t + 2)
                sp.wait_ge(lo_done, 12 * t + 12)
                vdst = v_dram.rearrange("(b h) p (u k) e -> b u p h (k e)", b=B, u=2)
                sp.dma_start(vdst[ds(t // 2, 1), ds(t % 2, 1)].rearrange("b u p h e -> p (b u h) e"),
                             v_st[:, :, :, :].rearrange("p h k e -> p h (k e)")).then_inc(v_stored, 16)
                if has_next(t):
                    sp.wait_ge(rounded, t + 1)
                    load_ffn_weights(t + 1)

            over_tiles(sp, tile)
            for i in range(4):
                sp.wait_ge(qk_stored[i], 16 * 2 * NT)
            sp.wait_ge(v_stored, 16 * NT)
            sp.wait_ge(xt_stored, 16 * 2 * NT)

        @block.gpsimd
        def _(pool):
            nc.gpsimd.memset(ident[:, :], 0.0).then_inc(ident_zero, 1)
            pool.wait_ge(ident_zero, 1)
            nc.gpsimd.affine_select(out=ident[:, :], in_=ident[:, :], compare_op=ALU.not_equal, fill=1.0, base=0,
                                    pattern=[[-1, P]], channel_multiplier=1).then_inc(ident_set, 1)
            nc.gpsimd.memset(v_st[:, :, :, 2 * DK:VE], 1.0).then_inc(ones_set, 1)

            def x_low(t):
                pool.wait_ge(xhi_done, t + 1)
                wait(pool, xt_mm, 4 * t)
                nc.gpsimd.tensor_tensor(x_part[:, LO, :, :], xn[:, :, :], x_part[:, HI, :, :],
                                        ALU.subtract).then_inc(xlo_done, 1)

            def largest_weight(m):
                pool.wait_ge(wmax_done, m + 1)
                nc.gpsimd.partition_all_reduce(w_gmax[:, m:m + 1], w_max[:, m:m + 1], P, RMAX).then_inc(wgmax_done, 1)

            largest_weight(0)
            x_low(0)
            largest_weight(1)
            largest_weight(2)
            x_low(1)
            largest_weight(3)
            with pool.Fori(2, NT) as t:
                x_low(t)
            pool.wait_ge(ffmax_done, 1)
            nc.gpsimd.partition_all_reduce(ff4g[:, :], ff4[:, :], P, RMAX).then_inc(ffg_done, 1)

        def pair_of_pieces(n):
            return bank[(0, 1, 6, 7)[n]][:, :].bitcast(F16).rearrange("p (k o) -> p k o", k=2)

        @block.scalar
        def _(act):
            def x_high(t):
                act.wait_ge(xn_done, t + 1)
                wait(act, xt_mm, 4 * t)
                nc.scalar.copy(x_part[:, HI, :, :], xn[:, :, :]).then_inc(xhi_done, 1)

            def copy_weights(m):
                for n in (0, 2):
                    act.wait_ge(wt_mm, 4 * m + n + 1)
                    nc.scalar.copy(w_t[m][:, n // 2, 0:2, :], pair_of_pieces(n)).then_inc(wt_act, 1)

            def weights_high(m):
                act.wait_ge(winv_done, m + 1)
                wait(act, wt_mm, 4 * (m - 1))
                nc.scalar.activation(w_part[m % 2][:, HI, :, :], w_raw[m][:, :, :], ACT.Copy,
                                     scale=w_inv[:, m:m + 1]).then_inc(w_hi_done, 1)

            def copy_x(t, par):
                for n in (0, 2):
                    act.wait_ge(xt_mm, 4 * t + n + 1)
                    wait(act, xt_stored, 32 * (t - 1))
                    nc.scalar.copy(x_t[par][:, n // 2, 0:2, :], pair_of_pieces(n)).then_inc(xt_act, 1)

            weights_high(0)
            copy_weights(0)
            x_high(0)
            copy_x(0, 0)
            weights_high(1)

            def tile(t, par):
                for c in range(12):
                    for m in WEIGHTS_COPIED.get((t, c), ()) if isinstance(t, int) else ():
                        copy_weights(m)
                    act.wait_ge(proj_mm, 12 * t + c + 1)
                    if c < 8:
                        wait(act, qk_stored[c % 4], 16 * (2 * t + c // 4))
                        nc.scalar.copy(qk_st[c % 4][:, HI, :], bank[2 + c % 4][:, :]).then_inc(hi_done, 1)
                    else:
                        wait(act, v_stored, 16 * t)
                        nc.scalar.copy(v_st[:, :, c - 8, DK:2 * DK],
                                       bank[2 + c % 4][:, :].rearrange("p (h d) -> p h d", d=DK)).then_inc(hi_done, 1)
                    for m in WEIGHTS_SPLIT.get((t, c), ()) if isinstance(t, int) else ():
                        weights_high(m)
                    if c == (7 if isinstance(t, int) and t == 0 else 4) and has_next(t):
                        x_high(t + 1)
                    if c == X_TURNED and has_next(t):
                        copy_x(t + 1, 1 - par)

            over_tiles(act, tile)

        @block.vector
        def _(dve):
            def link(ins, n):
                ins.then_inc(ln_link, 1)
                dve.wait_ge(ln_link, n)

            def norm_statistics(t):
                dve.wait_ge(x_loaded, 16 * (t + 1))
                for i in range(NB):
                    last = nc.vector.bn_stats(stats[:, i, :], x_in[:, i, :])
                last.then_inc(ln_link, 1)
                wait_apart(dve, ln_link, LINKS * t + 1, waits_apart)
                for i in range(NB):
                    last = nc.vector.bn_aggr(mv[:, i, :], stats[:, i, :])
                link(last, LINKS * t + 2)

            def norm_factor(t):
                n = LINKS * t + 3
                link(nc.vector.tensor_scalar(var[:, :], mv[:, :, 1], EPS, None, ALU.add), n)
                link(nc.vector.tensor_scalar(rstd[:, :].bitcast(I32), var[:, :].bitcast(I32), -0.5, GUESS,
                                             ALU.mult, ALU.add), n + 1)
                for i in range(NEWTON):
                    n = LINKS * t + 5 + 4 * i
                    link(nc.vector.tensor_tensor(nt0[:, :], rstd[:, :], rstd[:, :], ALU.mult), n)
                    link(nc.vector.tensor_tensor(nt1[:, :], nt0[:, :], var[:, :], ALU.mult), n + 1)
                    link(nc.vector.tensor_scalar(nt0[:, :], nt1[:, :], -0.5, 1.5, ALU.mult, ALU.add), n + 2)
                    link(nc.vector.tensor_tensor(rstd[:, :], rstd[:, :], nt0[:, :], ALU.mult), n + 3)

            def normalise(t):
                wait(dve, xhi_done, t)
                wait(dve, xlo_done, t)
                for i in range(NB):
                    last = nc.vector.tensor_scalar(xn[:, i, :], x_in[:, i, :], mv[:, i, 0:1], rstd[:, i:i + 1],
                                                   ALU.subtract, ALU.mult)
                last.then_inc(xn_done, 1)

            def copy_weights(m):
                for n in (1, 3):
                    dve.wait_ge(wt_mm, 4 * m + n + 1)
                    nc.vector.tensor_copy(w_t[m][:, n // 2, 2:4, :], pair_of_pieces(n)).then_inc(wt_dve, 1)

            def step(ins, n):
                ins.then_inc(fin_link, 1)
                dve.wait_ge(fin_link, n)

            def weights_max(m):
                dve.wait_ge(w_loaded[m], 16)
                nc.vector.tensor_reduce(w_max[:, m:m + 1], w_raw[m][:, :, :], AX.XY, ALU.max,
                                        apply_absolute_value=True).then_inc(wmax_done, 1)

            def weights_power(m):
                at = slice(m, m + 1)
                dve.wait_ge(wgmax_done, m + 1)
                nc.vector.tensor_scalar(w_gmax[:, at], w_gmax[:, at], 2.0 ** -50, 2.0 ** 50, ALU.max, ALU.min
                                        ).then_inc(pow_link, 1)
                dve.wait_ge(pow_link, 2 * m + 1)
                nc.vector.tensor_scalar(w_pow[:, at].bitcast(U32), w_gmax[:, at].bitcast(U32), EXP_BITS, None,
                                        ALU.bitwise_and).then_inc(pow_link, 1)
                dve.wait_ge(pow_link, 2 * m + 2)
                nc.vector.reciprocal(w_inv[:, at], w_pow[:, at]).then_inc(winv_done, 1)

            def weights_low(m):
                dve.wait_ge(w_hi_done, m + 1)
                nc.vector.scalar_tensor_tensor(w_part[m % 2][:, LO, :, :].rearrange("p c k -> p (c k)"),
                                               w_raw[m][:, :, :].rearrange("p c k -> p (c k)"), w_inv[:, m:m + 1],
                                               w_part[m % 2][:, HI, :, :].rearrange("p c k -> p (c k)"),
                                               ALU.mult, ALU.subtract).then_inc(w_lo_done, 1)

            def copy_x(t, par):
                for n in (1, 3):
                    dve.wait_ge(xt_mm, 4 * t + n + 1)
                    wait(dve, xt_stored, 32 * (t - 1))
                    nc.vector.tensor_copy(x_t[par][:, n // 2, 2:4, :], pair_of_pieces(n)).then_inc(xt_dve, 1)

            weights_max(0)
            weights_power(0)
            norm_statistics(0)
            weights_low(0)
            norm_factor(0)
            normalise(0)
            copy_weights(0)
            weights_max(1)
            weights_power(1)
            copy_x(0, 0)

            def round_weights(t, i):
                n = 3 * ROUND_LINKS * t + ROUND_LINKS * i
                part, mag = raw[:, i:i + 1, :], cmag[:, i:i + 1, :]
                dve.wait_ge(ffw_loaded, 48 * (t + 1))
                if i < 2:
                    nc.vector.tensor_reduce(ff_max[:, i, ds(t, 1)], part, AX.XY, ALU.max, apply_absolute_value=True)
                nc.vector.tensor_scalar(mag.bitcast(U32), part.bitcast(U32), EXP_BITS, None, ALU.bitwise_and
                                        ).then_inc(round_link, 1)
                dve.wait_ge(round_link, n + 1)
                nc.vector.tensor_scalar(mag, mag, 2.0 ** -6, 2.0 ** 119, ALU.max, ALU.mult).then_inc(round_link, 1)
                dve.wait_ge(round_link, n + 2)
                nc.vector.scalar_tensor_tensor(part, mag, 1.5 * 2.0 ** -99, part, ALU.mult, ALU.add
                                               ).then_inc(round_link, 1)
                dve.wait_ge(round_link, n + 3)
                if i < 2:
                    dst = (wg8, wu8)[i][:, :, :].rearrange("p k (h f) -> p (k h) f", h=2)[:, ds(t, 1), :]
                    nc.vector.scalar_tensor_tensor(dst, mag, -1.5 * 2.0 ** -99, part, ALU.mult, ALU.add)
                else:
                    nc.vector.scalar_tensor_tensor(
                        wd8[:, :, ds(t * DCOL, DCOL)], cmag[:, 2, :].rearrange("p (c o) -> p c o", c=FC),
                        -1.5 * 2.0 ** -99, raw[:, 2, :].rearrange("p (c o) -> p c o", c=FC),
                        ALU.mult, ALU.add).then_inc(rounded, 1)

            def feed_forward_factors():
                dve.wait_ge(small_loaded, 48)
                nc.vector.tensor_reduce(ff4[:, 0:2], ff_max[:, :, :], AX.X, ALU.max)
                nc.vector.tensor_reduce(ff4[:, 2:3], gs[:, :], AX.X, ALU.max, apply_absolute_value=True)
                nc.vector.tensor_reduce(ff4[:, 3:4], us[:, :], AX.X, ALU.max,
                                        apply_absolute_value=True).then_inc(ffmax_done, 1)
                dve.wait_ge(ffg_done, 1)
                step(nc.vector.tensor_scalar(bound[:, 0:2], ff4g[:, 0:2], 2.0 ** -9, 1.125 * D, ALU.add, ALU.mult), 4)
                step(nc.vector.tensor_tensor(bound[:, 0:2], bound[:, 0:2], ff4g[:, 2:4], ALU.mult), 5)
                step(nc.vector.tensor_tensor(bound[:, 2:3], bound[:, 0:1], bound[:, 1:2], ALU.mult), 6)
                step(nc.vector.tensor_scalar(bound[:, 2:3], bound[:, 2:3], 2.0 ** -50, 2.0 ** 100, ALU.max, ALU.min), 7)
                step(nc.vector.tensor_scalar(bound[:, 2:3].bitcast(U32), bound[:, 2:3].bitcast(U32), EXP_BITS, None,
                                             ALU.bitwise_and), 8)
                step(nc.vector.reciprocal(bound[:, 3:4], bound[:, 2:3]), 9)
                step(nc.vector.tensor_scalar(bound[:, 3:4], bound[:, 3:4], 2.0 ** 13, None, ALU.mult), 10)
                step(nc.vector.tensor_scalar(bound[:, 2:3], bound[:, 2:3], 2.0 ** -14, None, ALU.mult), 11)
                nc.vector.tensor_scalar(half_gs[:, :], gs[:, :], 0.5, None, ALU.mult)
                nc.vector.scalar_tensor_tensor(c_ff[:, :], gs[:, :], bound[:, 3:4], us[:, :], ALU.mult, ALU.mult)
                step(nc.vector.tensor_scalar(ds_row[:, :], ds_row[:, :], bound[:, 2:3], None, ALU.mult), 12)

            def factors_of_weights():
                step(nc.vector.tensor_tensor(s_exp[:, :], w_pow[:, 0:1], w_pow[:, 1:2], ALU.mult), 1)
                step(nc.vector.tensor_scalar(s_exp[:, :], s_exp[:, :], float(DK) ** -0.5, None, ALU.mult), 2)
                step(nc.vector.tensor_tensor(c_out[:, :], w_pow[:, 2:3], w_pow[:, 3:4], ALU.mult), 3)

            first_tile = {0: ("max 2",), 1: ("power 2",), 3: ("low 2",), 4: ("statistics",), 5: ("factor",),
                          6: ("normalise",), 7: ("round 0",), 8: ("round 1",), 9: ("round 2",)}
            second_tile = {0: ("statistics",), 1: ("factor",), 2: ("normalise", "max 3"), 3: ("power 3",),
                           4: ("low 3",), 5: ("round 0",), 7: ("round 1",), 8: ("round 2",)}
            other_tile = {0: ("statistics",), 1: ("factor",), 2: ("normalise",), 4: ("round 0",),
                          6: ("round 1",), 8: ("round 2",)}

            def tile(t, par):
                peeled = isinstance(t, int)
                plan = first_tile if peeled and t == 0 else second_tile if peeled and t == 1 else other_tile
                for c in range(12):
                    for m in WEIGHTS_COPIED.get((t, c), ()) if peeled else ():
                        copy_weights(m)
                    if peeled and t == c == 0:
                        weights_low(1)
                    dve.wait_ge(hi_done, 12 * t + c + 1)
                    src = bank[2 + c % 4][:, :]
                    if c < 8:
                        nc.vector.tensor_tensor(qk_st[c % 4][:, LO, :], src, qk_st[c % 4][:, HI, :],
                                                ALU.subtract).then_inc(lo_done, 1)
                    else:
                        at = v_st[:, :, c - 8, :]
                        nc.vector.tensor_tensor(at[:, :, 0:DK], src.rearrange("p (h d) -> p h d", d=DK),
                                                at[:, :, DK:2 * DK], ALU.subtract).then_inc(lo_done, 1)
                    for what in plan.get(c, ()):
                        name, _, m = what.partition(" ")
                        if name == "max":
                            weights_max(int(m))
                        elif name == "power":
                            weights_power(int(m))
                            if m == "3":
                                factors_of_weights()
                        elif name == "low":
                            weights_low(int(m))
                        elif name == "round":
                            round_weights(t, int(m))
                        elif has_next(t):
                            {"statistics": norm_statistics, "factor": norm_factor, "normalise": normalise}[name](t + 1)
                    if c == X_TURNED and has_next(t):
                        copy_x(t + 1, 1 - par)
                    if peeled and t == NT - 1 and c == 9:
                        feed_forward_factors()

            over_tiles(dve, tile)

        @block.tensor
        def _(pe):
            def fill(n, part, signal):
                dst = pair_of_pieces(n)
                for k in range(2):
                    for i in range(4):
                        kc = 2 * (n % 2) + k
                        mm = nc.tensor.transpose(dst[:, k, i * P:(i + 1) * P],
                                                 part[:, n // 2, i, kc * P:(kc + 1) * P], ident[:, :])
                mm.then_inc(signal, 1)

            def turn_weights(m, tiles):
                for n in range(4):
                    pe.wait_ge(w_hi_done if n < 2 else w_lo_done, m + 1)
                    wait(pe, wt_act if n % 2 == 0 else wt_dve, 2 * m + n // 2 - 1)
                    wait(pe, xt_act if n % 2 == 0 else xt_dve, 2 * tiles)
                    fill(n, w_part[m % 2], wt_mm)

            def turn_x(t, matrices):
                for n in range(4):
                    pe.wait_ge(xhi_done if n < 2 else xlo_done, t + 1)
                    wait(pe, wt_act if n % 2 == 0 else wt_dve, 2 * matrices - 1 + n // 2 if matrices == 1 else
                         2 * matrices)
                    wait(pe, xt_act if n % 2 == 0 else xt_dve, 2 * t + n // 2 - 1)
                    fill(n, x_part, xt_mm)

            pe.wait_ge(ident_set, 1)
            turn_weights(0, 0)
            turn_x(0, 1)

            def tile(t, par):
                for c in range(12):
                    if c == 0:
                        pe.wait_ge(xt_act, 2 * t + 2)
                        pe.wait_ge(xt_dve, 2 * t + 2)
                    if c % 4 == 0 and isinstance(t, int) and t == 0:
                        pe.wait_ge(wt_act, 2 * (c // 4 + 1))
                        pe.wait_ge(wt_dve, 2 * (c // 4 + 1))
                    wait(pe, lo_done, 12 * t + c - 3)
                    first = True
                    for wp, xp in TERMS:
                        for kc in range(KC):
                            if c < 8:
                                o = c % 4
                                lhs, rhs = w_t[c // 4][:, wp, kc, o * P:(o + 1) * P], x_t[par][:, xp, kc, :]
                            else:
                                i = c - 8
                                lhs, rhs = x_t[par][:, xp, kc, i * P:(i + 1) * P], w_t[2][:, wp, kc, :]
                            mm = nc.tensor.matmul(bank[2 + c % 4][:, :], lhs, rhs, start=first,
                                                  stop=((wp, xp) == TERMS[-1] and kc == KC - 1))
                            first = False
                    mm.then_inc(proj_mm, 1)
                    for m in WEIGHTS_COPIED.get((t, c + 1), ()) if isinstance(t, int) else ():
                        turn_weights(m, t + 1)
                    if c == X_TURNED - 1 and has_next(t):
                        turn_x(t + 1, 3 if isinstance(t, int) and t == 0 else 4)

            over_tiles(pe, tile)


def attend(nc, x, out, q_dram, k_dram, v_dram, xn_dram, keep, bank):
    wo_t, wg8, wu8, wd8, ident, s_exp, c_out, half_gs, c_ff, ds_row = (
        keep[n] for n in ("wo_t", "wg8", "wu8", "wd8", "ident", "s_exp", "c_out", "half_gs", "c_ff", "ds_row"))
    x_v = x.rearrange("b (i p) d -> (b i) p d", p=P)
    out_v = out.rearrange("b (i p) d -> (b i) p d", p=P)
    with ExitStack() as ctx:
        def sb(name, shape, dt):
            return ctx.enter_context(nc.sbuf_tensor(name, shape, dt))

        def sem(name):
            return ctx.enter_context(nc.semaphore(name))

        q_st = [sb(f"q_st{i}", [3 * DK + 2, S], F16) for i in range(4)]
        k_st = [sb(f"k_st{i}", [3 * DK + 2, S], F16) for i in range(4)]
        v_sb = [sb(f"v_sb{i}", [P, QB, VE], F16) for i in range(4)]
        p32 = [sb(f"p32_{i}", [P, 512], F32) for i in range(RING)]
        probs = [sb(f"probs{i}", [P, 2, NE * 512], F16) for i in range(2)]
        mask = sb("mask", [P, 512], F32)
        junk = [sb(f"junk{i}", [P, 512], mybir.dt.bfloat16) for i in range(2)]
        mx = sb("mx", [P, 12], F32)
        m_part = sb("m_part", [P, 16], F16)
        m_row = [sb(f"m_row{i}", [16, P], F16) for i in range(2)]
        rsum = sb("rsum", [P, QB // 2], F32)
        o_low = sb("o_low", [P, QB // 2, DK], F32)
        o_sum = sb("o_sum", [P, QB // 2, DK], F32)
        attn = sb("attn", [P, 2, QB, D], F32)
        a_part = sb("a_part", [P, 2, D], F16)
        a_t = sb("a_t", [P, 2, KC, P], F16)
        xt = sb("xt", [P, 2, KC, FT], F16)
        th = [sb(f"th{i}", [P, FT], F32) for i in range(2)]
        ga = sb("ga", [P, FT], F32)
        fu = [sb(f"fu{i}", [P, FT], F32) for i in range(FU)]
        fuse = sb("fuse", [P, 2, FC, FT], F16)
        ff_out = sb("ff_out", [P, D], F32)
        res = sb("res", [P, QB, D], F32)
        o_sb = [sb(f"o_sb{i}", [P, D], F32) for i in range(2)]

        st_bank, m_bank = bank[0:2], bank[2:4]
        o_bank, ff_bank, misc = bank[4], bank[5:7], bank[7]
        o_half = o_bank[:, 0:QB // 2 * VN].rearrange("p (i e) -> p i e", e=VN)

        q_loaded = [sem(f"q_loaded{i}") for i in range(4)]
        v_loaded = [sem(f"v_loaded{i}") for i in range(4)]
        row_loaded = [sem(f"row_loaded{i}") for i in range(4)]
        xt_loaded = sem("xt_loaded")
        xb_loaded = sem("xb_loaded")
        out_stored = [sem(f"out_stored{i}") for i in range(2)]
        ones_set = sem("ones_set2")
        mask_zero = sem("mask_zero")
        mask_set = sem("mask_set")
        m_mm = sem("m_mm")
        m_red = sem("m_red")
        m_link = sem("m_link")
        mt_mm = sem("mt_mm")
        mt_copied = sem("mt_copied")
        e_mm = sem("e_mm")
        exp_done = sem("exp_done")
        diag_done = sem("diag_done")
        p_hi = sem("p_hi")
        p_lo_dve = sem("p_lo_dve")
        p_lo_pool = sem("p_lo_pool")
        pv_mm = sem("pv_mm")
        o_link = sem("o_link")
        o_done = sem("o_done")
        ff_mm = sem("ff_mm")
        tanh_done = sem("tanh_done")
        ga_done = sem("ga_done")
        fu_done = sem("fu_done")
        fuse_hi = sem("fuse_hi")
        fuse_lo = sem("fuse_lo")
        down_mm = sem("down_mm")
        dn_link = sem("dn_link")
        res_done = sem("res_done")
        split_link = sem("split_link")
        split_done = sem("split_done")
        turn_mm = sem("turn_mm")
        turned = sem("turned")
        op_mm = sem("op_mm")
        o_ready = sem("o_ready")
        dve_waits = sem("dve_waits")
        pool_waits = sem("pool_waits")
        block = ctx.enter_context(nc.Block())

        def over_iterations(eng, step):
            step(0, False)
            with eng.Fori(1, LAG) as it:
                step(it, False)
            with eng.Fori(LAG, NIT) as it:
                step(it, True)

        def load_head(sp, n, i):
            for dst, dram, rows in ((q_st[i], q_dram, (HI, LO, HI)), (k_st[i], k_dram, (HI, HI, LO))):
                for r, w in enumerate(rows):
                    sp.dma_start(dst[r * DK:(r + 1) * DK, :], dram[w, ds(n, 1)].rearrange("a d t -> (a d) t")
                                 ).then_inc(q_loaded[i], 16)

        def load_v(sp, n, i):
            sp.dma_start(v_sb[i][:, :, :], v_dram[ds(n, 1)].rearrange("a p k e -> p (a k) e")
                         ).then_inc(v_loaded[i], 16)

        def take_low(eng, ops, units, it, k, signal):
            if k % NE not in units or (isinstance(it, int) and it == 0 and k < 0):
                return
            s, u = k // NE, k % NE
            at = slice(u * 512, (u + 1) * 512)
            eng.wait_ge(p_hi, STEPS * it + k + 1)
            ops.tensor_tensor(probs[s % 2][:, LO, at], p32[k % RING][:, :], probs[s % 2][:, HI, at],
                              ALU.subtract).then_inc(signal, 1)

        late_part = [probs[0][:, HI, i * 2 * D:(i + 1) * 2 * D].rearrange("p (w d) -> p w d", w=2)
                     for i in range(2)]
        late_t = [probs[0][:, LO, i * 2 * D:(i + 1) * 2 * D].rearrange("p (w k t) -> p w k t", w=2, k=KC)
                  for i in range(2)]

        def attention_rows(i, r):
            return attn[:, ds((r // 4) % 2, 1), ds((r % 4) * 2 + i, 1), :].rearrange("p a i d -> p (a i d)")

        @block.sync
        def _(sp):
            def load_tile(t):
                sp.dma_start(xt[:, :, :, :].rearrange("p w k t -> p (w k) t"),
                             xn_dram[ds(t, 1)].rearrange("a p w k t -> p (a w k) t")).then_inc(xt_loaded, 16)

            def store_row(i, m):
                sp.wait_ge(mt_copied, m)
                sp.dma_start(q_st[i][3 * DK:3 * DK + 2, :], m_row[i % 2][:, :]).then_inc(row_loaded[i], 16)

            for i in range(2):
                sp.sem_inc(out_stored[i], 16)
            for n in range(3):
                load_head(sp, n, n)
                if n < 2:
                    load_v(sp, n, n)
            load_tile(0)
            store_row(0, 1)

            def iteration(it, with_out):
                for s in range(HEADS_PER_IT):
                    n = 4 * it + s
                    wait(sp, e_mm, NE * n)
                    load_head(sp, (n + 3) % NH, (s + 3) % 4)
                    wait(sp, pv_mm, 2 * (n - 1))
                    load_v(sp, (n + 2) % NH, (s + 2) % 4)
                    if with_out and s in (2, 3):
                        store_out(2 * (it - LAG) + s - 2, s - 2, it - LAG)
                    if s == 3:
                        sp.dma_start(res[:, ds(it % 4 * 2, 2), :],
                                     x_v[ds(2 * it, 2)].rearrange("a p d -> p a d")).then_inc(xb_loaded, 16)
                    store_row((s + 1) % 4, n + 2)
                    if s == 3:
                        sp.wait_ge(ff_mm, FC * (it + 1))
                        load_tile((it + 1) % NIT)

            def store_out(b, i, r):
                sp.wait_ge(o_ready, 2 * r + i + 1)
                sp.dma_start(out_v[ds(b, 1)].rearrange("a p d -> p (a d)"), o_sb[i][:, :]).then_inc(out_stored[i], 16)

            over_iterations(sp, iteration)
            with sp.Fori(NIT - LAG, NIT) as r:
                for i in range(2):
                    store_out(2 * r + i, i, r)
            for i in range(2):
                sp.wait_ge(out_stored[i], 16 * (NIT + 1))
                sp.wait_ge(row_loaded[i], 16 * (NIT + (i == 0)))
            for i in range(4):
                sp.wait_ge(q_loaded[i], 96 * (NIT + (i < 3)))
                sp.wait_ge(v_loaded[i], 16 * (NIT + (i < 2)))
            sp.wait_ge(xt_loaded, 16 * (NIT + 1))

        @block.gpsimd
        def _(pool):
            nc.gpsimd.memset(mask[:, :], 0.0).then_inc(mask_zero, 1)
            pool.wait_ge(mask_zero, 1)
            nc.gpsimd.affine_select(out=mask[:, 512 - P:512], in_=mask[:, 512 - P:512], compare_op=ALU.is_ge,
                                    fill=MASKED, base=0, pattern=[[-1, P]], channel_multiplier=1
                                    ).then_inc(mask_set, 1)

            def add_down(i, t):
                at = res[:, ds(t % 4 * 2 + i, 1), :].rearrange("p a d -> p (a d)")
                pool.wait_ge(dn_link, 2 * t + i + 1)
                pool.wait_ge(xb_loaded, 16 * (t + 1))
                nc.gpsimd.tensor_tensor(at, ff_out[:, :], at, ALU.add).then_inc(res_done, 1)

            def low_of_attention(i, r, part, rows):
                pool.wait_ge(split_link, 2 * r + i + 1)
                nc.gpsimd.tensor_tensor(part[:, LO, :], rows, part[:, HI, :], ALU.subtract).then_inc(split_done, 1)

            def low_of_fuse(f, t):
                pool.wait_ge(fuse_hi, FC * t + f + 1)
                nc.gpsimd.tensor_tensor(fuse[:, LO, f, :], fu[f % FU][:, :], fuse[:, HI, f, :],
                                        ALU.subtract).then_inc(fuse_lo, 1)

            def iteration(it, with_out):
                for s in range(HEADS_PER_IT):
                    for u in range(NE):
                        if u in DIAGONAL:
                            wait_apart(pool, exp_done, NE * (4 * it + s) + u + 1, pool_waits)
                            blocks = 2 if DIAGONAL[u] else 1
                            step = DIAGONAL[u] or P
                            at = p32[(s * NE + u) % RING][:, :].rearrange("p (b q) -> p b q", q=P)
                            at = at[:, 0:(blocks - 1) * (step // P) + 1:step // P, :]
                            nc.gpsimd.affine_select(out=at, in_=at, compare_op=ALU.is_ge, fill=0.0, base=0,
                                                    pattern=[[0, blocks], [1, P]], channel_multiplier=-1
                                                    ).then_inc(diag_done, 1)
                        take_low(pool, nc.gpsimd, POOL_LOW, it, s * NE + u - 2, p_lo_pool)
                        for f, ti in at_step(FUSE_STEP, it, s * NE + u):
                            low_of_fuse(f, ti)
                        if s * NE + u in ADD_DOWN_STEP and not isinstance(it, int):
                            add_down(ADD_DOWN_STEP[s * NE + u], it - 1)
                        if with_out and s * NE + u - 1 in SPLIT_STEP:
                            i, r = SPLIT_STEP[s * NE + u - 1], it - LAG
                            low_of_attention(i, r, a_part, attention_rows(i, r))

            over_iterations(pool, iteration)
            for k in (STEPS - 2, STEPS - 1):
                take_low(pool, nc.gpsimd, POOL_LOW, NIT - 1, k, p_lo_pool)
            for k in range(STEPS, STEPS + 3):
                for f, t in at_step(FUSE_STEP, NIT - 1, k):
                    low_of_fuse(f, t)
            for i in range(2):
                add_down(i, NIT - 1)
            with pool.Fori(NIT - LAG, NIT) as r:
                for i in range(2):
                    low_of_attention(i, r, late_part[i], attention_rows(i, r))

        @block.scalar
        def _(act):
            def take_high(it, k):
                if isinstance(it, int) and it == 0 and k < 0:
                    return
                s, u = k // NE, k % NE
                act.wait_ge(exp_done, STEPS * it + k + 1)
                if u in DIAGONAL:
                    act.wait_ge(diag_done, ND * (HEADS_PER_IT * it + s) + sorted(DIAGONAL).index(u) + 1)
                if u == 0:
                    wait(act, pv_mm, 2 * (HEADS_PER_IT * it + s - 1))
                nc.scalar.copy(probs[s % 2][:, HI, u * 512:(u + 1) * 512], p32[k % RING][:, :]).then_inc(p_hi, 1)

            def tanh_of_gate(f, t):
                g = FC * t + f
                act.wait_ge(ff_mm, g + 1)
                wait(act, ga_done, g - 1)
                nc.scalar.activation(th[f % 2][:, :], ff_bank[f % 2][:, 0:FT], ACT.Tanh,
                                     scale=half_gs[:, f:f + 1]).then_inc(tanh_done, 1)

            def high_of_fuse(f, t):
                act.wait_ge(fu_done, FC * t + f + 1)
                if f == 0:
                    wait(act, down_mm, 2 * t)
                nc.scalar.copy(fuse[:, HI, f, :], fu[f % FU][:, :]).then_inc(fuse_hi, 1)

            def iteration(it, with_out):
                for s in range(HEADS_PER_IT):
                    n = HEADS_PER_IT * it + s
                    for u in range(NE):
                        k = s * NE + u
                        e = NE * n + u
                        act.wait_ge(e_mm, e + 1)
                        old = k - RING
                        if old % NE in POOL_LOW:
                            wait(act, p_lo_pool, HEADS_PER_IT * len(POOL_LOW) * it + low_parts(POOL_LOW, old))
                        else:
                            wait(act, p_lo_dve, HEADS_PER_IT * len(DVE_LOW) * it + low_parts(DVE_LOW, old))
                        nc.scalar.activation(p32[k % RING][:, :], st_bank[(s + u) % 2][:, :],
                                             ACT.Exp, scale=s_exp[:, :]).then_inc(exp_done, 1)
                        take_high(it, k - 1)
                        for f, t in at_step(TANH_STEP, it, k):
                            tanh_of_gate(f, t)
                        if with_out and k - 1 in TURN_STEP:
                            act.wait_ge(turn_mm, 2 * (it - LAG) + TURN_STEP[k - 1] + 1)
                            nc.scalar.copy(a_t[:, :, :, :].rearrange("p w k t -> p (w k t)"),
                                           misc[:, :].bitcast(F16)).then_inc(turned, 1)
                        for f, t in at_step(FUSE_STEP, it, k):
                            high_of_fuse(f, t)
                        if with_out and k in SPLIT_STEP:
                            i, r = SPLIT_STEP[k], it - LAG
                            act.wait_ge(o_done, 2 * HEADS_PER_IT * it)
                            nc.scalar.copy(a_part[:, HI, :], attention_rows(i, r)).then_inc(split_link, 1)

            over_iterations(act, iteration)
            take_high(NIT - 1, STEPS - 1)
            for k in range(STEPS, STEPS + 3):
                for f, t in at_step(TANH_STEP, NIT - 1, k):
                    tanh_of_gate(f, t)
                for f, t in at_step(FUSE_STEP, NIT - 1, k):
                    high_of_fuse(f, t)
            act.wait_ge(o_done, 2 * NH)
            with act.Fori(NIT - LAG, NIT) as r:
                for i in range(2):
                    act.wait_ge(turn_mm, 2 * r + i - 1)
                    nc.scalar.copy(late_part[i][:, HI, :], attention_rows(i, r)).then_inc(split_link, 1)

        @block.vector
        def _(dve):
            def row_maxima(m, units):
                for u in units:
                    i, k0, w, col = M_UNITS[u]
                    if u == 0 and not (isinstance(m, int) and m == 0):
                        wait_apart(dve, m_link, 3 * m, dve_waits)
                    if k0 + w == (i + 1) * P:
                        wait_apart(dve, m_mm, NM * m + u + 1, dve_waits)
                    else:
                        dve.wait_ge(m_mm, NM * m + u + 1)
                    src = m_bank[u % 2][:, 0:w]
                    if k0 + w == (i + 1) * P:
                        ins = nc.vector.tensor_tensor_reduce(
                            out=junk[u % 2][:, 0:w], in0=src, in1=mask[:, 512 - w:512], scale=1.0, scalar=MASKED,
                            op0=ALU.add, op1=ALU.max, accum_out=mx[:, col:col + 1])
                    else:
                        ins = nc.vector.tensor_reduce(mx[:, col:col + 1], src, AX.X, ALU.max)
                    ins.then_inc(m_red, 1)

            def split_maxima(m):
                dve.wait_ge(m_red, NM * (m + 1))
                nc.vector.tensor_tensor(mx[:, 4:8], mx[:, 4:8], mx[:, 8:12], ALU.max).then_inc(m_link, 1)
                dve.wait_ge(m_link, 3 * m + 1)
                wait(dve, mt_mm, m)
                nc.vector.tensor_scalar(m_part[:, 0:8], mx[:, 0:8], -1.0 / MSCALE, None, ALU.mult
                                        ).then_inc(m_link, 1)
                dve.wait_ge(m_link, 3 * m + 2)
                nc.vector.scalar_tensor_tensor(m_part[:, 8:16], mx[:, 0:8], -1.0 / MSCALE, m_part[:, 0:8],
                                               ALU.mult, ALU.subtract).then_inc(m_link, 1)

            def copy_row(m, i, last_use):
                dve.wait_ge(mt_mm, m + 1)
                wait(dve, row_loaded[(i + 2) % 4], 16 * last_use)
                nc.vector.tensor_copy(m_row[i % 2][:, :], misc[0:16, 0:P // 2].bitcast(F16)
                                      ).then_inc(mt_copied, 1)

            def normalise(n, half):
                batch, head = n // H, n % H
                dve.wait_ge(pv_mm, 2 * n + half + 1)
                nc.vector.tensor_copy(o_low[:, :, :], o_half[:, :, 0:DK])
                nc.vector.reciprocal(rsum[:, :], o_half[:, :, 2 * DK]).then_inc(o_link, 1)
                dve.wait_ge(o_link, 4 * n + 2 * half + 1)
                nc.vector.tensor_tensor(o_sum[:, :, :], o_half[:, :, DK:2 * DK], o_low[:, :, :],
                                        ALU.add).then_inc(o_link, 1)
                dve.wait_ge(o_link, 4 * n + 2 * half + 2)
                blocks = slice(half * QB // 2, (half + 1) * QB // 2)
                dst = attn[:, ds(batch % 2, 1), blocks, ds(head * DK, DK)].rearrange("p a i d -> p (a i) d")
                nc.vector.tensor_tensor(dst, o_sum[:, :, :],
                                        rsum[:, :].unsqueeze(2).broadcast_to([P, QB // 2, DK]),
                                        ALU.mult).then_inc(o_done, 1)

            def copy_turned(i, r):
                dve.wait_ge(turn_mm, 2 * r + i + 1)
                dve.wait_ge(op_mm, 2 * r + i - 1)
                nc.vector.tensor_copy(late_t[i].rearrange("p w k t -> p (w k t)"),
                                      bank[i][:, :].bitcast(F16)).then_inc(turned, 1)

            def add_output(i, r, src=misc):
                dve.wait_ge(op_mm, 2 * r + i + 1)
                dve.wait_ge(out_stored[i], 16 * (r + 1))
                blk = (r % 4) * 2 + i
                nc.vector.scalar_tensor_tensor(
                    o_sb[i][:, :], src[:, :], c_out[:, 0:1],
                    res[:, ds(blk, 1), :].rearrange("p a d -> p (a d)"), ALU.mult, ALU.add).then_inc(o_ready, 1)

            def scale_down(i, t):
                dve.wait_ge(down_mm, 2 * t + i + 1)
                wait(dve, res_done, 2 * t + i)
                nc.vector.tensor_tensor(ff_out[:, :], misc[:, :], ds_row[:, :], ALU.mult).then_inc(dn_link, 1)

            def swiglu(f, t):
                g = FC * t + f
                dve.wait_ge(tanh_done, g + 1)
                wait(dve, fu_done, g)
                nc.vector.scalar_tensor_tensor(ga[:, :], th[f % 2][:, :], 1.0, ff_bank[f % 2][:, 0:FT],
                                               ALU.add, ALU.mult).then_inc(ga_done, 1)
                dve.wait_ge(ga_done, g + 1)
                wait(dve, fuse_lo, g - FU + 1)
                nc.vector.scalar_tensor_tensor(fu[f % FU][:, :], ff_bank[f % 2][:, FT:2 * FT], c_ff[:, f:f + 1],
                                               ga[:, :], ALU.mult, ALU.mult).then_inc(fu_done, 1)

            for i in range(4):
                last = nc.vector.memset(k_st[i][3 * DK:3 * DK + 2, :], MSCALE)
            last.then_inc(ones_set, 1)
            dve.wait_ge(mask_set, 1)
            row_maxima(0, range(NM))
            split_maxima(0)
            copy_row(0, 0, 0)
            row_maxima(1, range(NM))

            def iteration(it, with_out):
                for s in range(HEADS_PER_IT):
                    n = 4 * it + s
                    for u in range(NE):
                        k = s * NE + u
                        if u == 0:
                            split_maxima(n + 1)
                        if u == 4 and not (isinstance(it, int) and n == 0):
                            normalise(n - 1, 0)
                        for f, t in at_step(SWIGLU_STEP, it, k):
                            swiglu(f, t)
                        row_maxima(n + 2, M_STEP.get(u, ()))
                        take_low(dve, nc.vector, DVE_LOW, it, k - 2, p_lo_dve)
                        if k in ROW_STEP:
                            copy_row(n + 1, (s + 1) % 4, it if s == 0 else it + 1)
                        if u == NE - 1 and not (isinstance(it, int) and n == 0):
                            normalise(n - 1, 1)
                        if with_out and k in ADD_OUT_STEP:
                            add_output(ADD_OUT_STEP[k], it - LAG)
                        if k in ADD_DOWN_STEP and not isinstance(it, int):
                            scale_down(ADD_DOWN_STEP[k], it - 1)

            over_iterations(dve, iteration)
            for k in (STEPS - 2, STEPS - 1):
                take_low(dve, nc.vector, DVE_LOW, NIT - 1, k, p_lo_dve)
            for k in range(STEPS, STEPS + 3):
                for f, t in at_step(SWIGLU_STEP, NIT - 1, k):
                    swiglu(f, t)
            for half in range(2):
                normalise(NH - 1, half)
            for i in range(2):
                scale_down(i, NIT - 1)

            def last_iteration(r, more):
                copy_turned(1, r)
                add_output(0, r, bank[2])
                if more:
                    copy_turned(0, r + 1)
                add_output(1, r, bank[3])

            copy_turned(0, NIT - LAG)
            dve.wait_ge(res_done, 2 * NIT)
            with dve.Fori(NIT - LAG, NIT - 1) as r:
                last_iteration(r, True)
            last_iteration(NIT - 1, False)

        @block.tensor
        def _(pe):
            def maxima_scores(m, i, units):
                rows = slice(0, 3 * DK)
                for u in units:
                    blk, k0, w, _ = M_UNITS[u]
                    wait(pe, m_red, NM * m + u - 1)
                    nc.tensor.matmul(m_bank[u % 2][:, 0:w], q_st[i][rows, blk * P:(blk + 1) * P],
                                     k_st[i][rows, k0:k0 + w], start=True, stop=True).then_inc(m_mm, 1)

            def turn_maxima(m):
                pe.wait_ge(m_link, 3 * (m + 1))
                nc.tensor.transpose(misc[0:16, 0:P // 2].bitcast(F16), m_part[:, :], ident[:, :]
                                    ).then_inc(mt_mm, 1)

            def scores(n, s, u):
                e = NE * n + u
                wait(pe, exp_done, e - 1)
                at = 0
                for j, q0, w in E_UNITS[u]:
                    mm = nc.tensor.matmul(st_bank[(s + u) % 2][:, at:at + w], k_st[s][:, j * P:(j + 1) * P],
                                          q_st[s][:, q0:q0 + w], start=True, stop=True)
                    at += w
                mm.then_inc(e_mm, 1)

            def values(n, s, i):
                if i % (QB // 2) == 0:
                    wait(pe, o_done, 2 * n + i // (QB // 2))
                for j in range(i + 1):
                    at = p_column(j, i)
                    for part in (HI, LO):
                        mm = nc.tensor.matmul(o_half[:, i % (QB // 2), :], probs[s % 2][:, part, at:at + P],
                                              v_sb[s][:, j, 0:VN], start=(j == 0 and part == HI),
                                              stop=(j == i and part == LO))
                if i % (QB // 2) == QB // 2 - 1:
                    mm.then_inc(pv_mm, 1)

            def start_values(n, s, uses, units):
                if units < NE:
                    pe.wait_ge(v_loaded[s], 16 * uses)
                pe.wait_ge(p_lo_dve, len(DVE_LOW) * n + low_parts(DVE_LOW, units - 1))
                pe.wait_ge(p_lo_pool, len(POOL_LOW) * n + low_parts(POOL_LOW, units - 1))

            def feed_forward(h, f, it):
                if h == 0:
                    if f == 0:
                        pe.wait_ge(xt_loaded, 16 * (it + 1))
                    wait(pe, fu_done, FC * it + f - 1)
                for part in (HI, LO):
                    for kc in range(KC):
                        mm = nc.tensor.matmul(ff_bank[f % 2][:, h * FT:(h + 1) * FT],
                                              (wg8, wu8)[h][:, kc, f * P:(f + 1) * P], xt[:, part, kc, :],
                                              start=(part == HI and kc == 0), stop=(part == LO and kc == KC - 1))
                if h == 1:
                    mm.then_inc(ff_mm, 1)

            def down(i, piece, t):
                units = range(piece * FC // DOWN_PIECES, (piece + 1) * FC // DOWN_PIECES)
                if i == 0:
                    pe.wait_ge(fuse_lo, FC * t + units[-1] + 1)
                for f in units:
                    for part in (HI, LO):
                        mm = nc.tensor.matmul(misc[:, :], fuse[:, part, f, i * P:(i + 1) * P], wd8[:, f, :],
                                              start=(f == 0 and part == HI), stop=(f == FC - 1 and part == LO))
                if piece == DOWN_PIECES - 1:
                    mm.then_inc(down_mm, 1)

            def turn_attention(i, r, out=misc, src=a_part):
                pe.wait_ge(split_done, 2 * r + i + 1)
                dst = out[:, :].bitcast(F16).rearrange("p (w k t) -> p w k t", w=2, k=KC)
                for part in (HI, LO):
                    for kc in range(KC):
                        mm = nc.tensor.transpose(dst[:, part, kc, :], src[:, part, kc * P:(kc + 1) * P],
                                                 ident[:, :])
                mm.then_inc(turn_mm, 1)

            def project(i, piece, r, out=misc, src=a_t):
                if piece == 0:
                    pe.wait_ge(turned, 2 * r + i + 1)
                products = [(ap, wp, kc) for ap, wp in TERMS for kc in range(KC)]
                for m, (ap, wp, kc) in list(enumerate(products))[piece * 4:piece * 4 + 4]:
                    mm = nc.tensor.matmul(out[:, :], src[:, ap, kc, :], wo_t[:, wp, kc, :],
                                          start=(m == 0), stop=(m == len(products) - 1))
                if piece == PROJ_PIECES - 1:
                    mm.then_inc(op_mm, 1)

            pe.wait_ge(ones_set, 1)
            pe.wait_ge(q_loaded[0], 96)
            maxima_scores(0, 0, range(NM))
            turn_maxima(0)
            pe.wait_ge(q_loaded[1], 96)
            maxima_scores(1, 1, range(NM))

            def iteration(it, with_out):
                first = isinstance(it, int)
                r = it - LAG
                for s in range(HEADS_PER_IT):
                    n = 4 * it + s
                    for u in range(NE):
                        k = s * NE + u
                        if u == 0:
                            pe.wait_ge(row_loaded[s], 16 * (it + 1))
                        scores(n, s, u)
                        if u == 1:
                            pe.wait_ge(q_loaded[(s + 2) % 4], 96 * ((it + 1) if s < 2 else (it + 2)))
                        maxima_scores(n + 2, (s + 2) % 4, M_STEP.get(u, ()))
                        if not (first and n == 0):
                            if u in (1, 5):
                                start_values(n - 1, (s + 3) % 4, it if s == 0 else it + 1, 3 if u == 1 else NE)
                            for i in PV_STEP.get(u, ()):
                                values(n - 1, (s + 3) % 4, i)
                        if k in ROW_STEP:
                            if s in (0, 1) and not first:
                                pe.wait_ge(dn_link, 2 * it - 1 + s)
                            elif s in (2, 3) and with_out:
                                pe.wait_ge(o_ready, 2 * r + s - 1)
                            else:
                                pe.wait_ge(mt_copied, n + 1)
                            turn_maxima(n + 1)
                        if not first:
                            for i, piece in DOWN_STEP.get(k, ()):
                                if piece == 0:
                                    pe.wait_ge(mt_copied, 4 * it + 1 + i)
                                down(i, piece, it - 1)
                        if k in GATE_STEP:
                            feed_forward(0, GATE_STEP[k], it)
                        if k in UP_STEP:
                            feed_forward(1, UP_STEP[k], it)
                        if with_out:
                            if k in TURN_STEP:
                                pe.wait_ge(mt_copied, 4 * it + 3 + TURN_STEP[k])
                                turn_attention(TURN_STEP[k], r)
                            for i, piece in PROJ_STEP.get(k, ()):
                                project(i, piece, r)

            over_iterations(pe, iteration)
            start_values(NH - 1, 3, NIT, 3)
            start_values(NH - 1, 3, NIT, NE)
            for i in range(QB):
                values(NH - 1, 3, i)
            for i in range(2):
                pe.wait_ge(*((dn_link, 2 * NIT - 1) if i else (mt_copied, NH + 1)))
                for piece in range(DOWN_PIECES):
                    down(i, piece, NIT - 1)

            def last_turn(i, r):
                pe.wait_ge(turned, 2 * r + i - 1)
                turn_attention(i, r, bank[i], late_part[i])

            def last_project(i, r):
                pe.wait_ge(o_ready, 2 * r + i - 1)
                for piece in range(PROJ_PIECES):
                    project(i, piece, r, bank[2 + i], late_t[i])

            def last_iteration(r, more):
                last_turn(1, r)
                last_project(0, r)
                if more:
                    last_turn(0, r + 1)
                last_project(1, r)

            pe.wait_ge(m_red, NM * (NH + 2))
            last_turn(0, NIT - LAG)
            with pe.Fori(NIT - LAG, NIT - 1) as r:
                last_iteration(r, True)
            last_iteration(NIT - 1, False)


def build(nc, x, wq, wk, wv, wo, gate_w, up_w, down_w, gate_s, up_s, down_s, out):
    q_dram = nc.dram_tensor("q_parts", (2, NH, DK, S), F16, kind="Internal").ap()
    k_dram = nc.dram_tensor("k_parts", (2, NH, DK, S), F16, kind="Internal").ap()
    v_dram = nc.dram_tensor("v_parts", (NH, P, QB, VE), F16, kind="Internal").ap()
    xn_dram = nc.dram_tensor("xn_parts", (NIT, P, 2, KC, FT), F16, kind="Internal").ap()
    with ExitStack() as ctx:
        def sb(name, shape, dt):
            return ctx.enter_context(nc.sbuf_tensor(name, shape, dt))

        bank = [ctx.enter_context(nc.psum_tensor(f"bank{i}", [P, 512], F32)) for i in range(8)]
        keep = {"wo_t": sb("wo_t", [P, 2, KC, D], F16), "wg8": sb("wg8", [P, KC, INNER], F16),
                "wu8": sb("wu8", [P, KC, INNER], F16), "wd8": sb("wd8", [P, FC, D], F16),
                "ident": sb("ident", [P, P], F16), "s_exp": sb("s_exp", [P, 1], F32),
                "c_out": sb("c_out", [P, 1], F32), "half_gs": sb("half_gs", [P, FC], F32),
                "c_ff": sb("c_ff", [P, FC], F32), "ds_row": sb("ds_row", [P, D], F32)}
        prepare(nc, x, (wq, wk, wv, wo), (gate_w, up_w, down_w), (gate_s, up_s, down_s),
                q_dram, k_dram, v_dram, xn_dram, keep, bank)
        attend(nc, x, out, q_dram, k_dram, v_dram, xn_dram, keep, bank)


_INS = ["L0_attn_x", "L0_attn_Wq", "L0_attn_Wk", "L0_attn_Wv", "L0_attn_Wo", "L0_ffn_gate_w", "L0_ffn_up_w",
        "L0_ffn_down_w", "L0_ffn_gate_scale", "L0_ffn_up_scale", "L0_ffn_down_scale"]


def kernel(**inputs):
    import numpy as _np
    import concourse.bacc as _bacc
    from concourse import mybir as _mybir
    from concourse.bass_utils import run_bass_kernel_spmd as _run

    nc = _bacc.Bacc("TRN2", target_bir_lowering=False, num_devices=1)
    arrays, args = {}, []
    for name in _INS:
        a = _np.ascontiguousarray(inputs[name])
        arrays[f"in_{name}"] = a
        args.append(nc.dram_tensor(f"in_{name}", a.shape, _mybir.dt.from_np(a.dtype), kind="ExternalInput").ap())
    args.append(nc.dram_tensor("out_0", (B, S, D), F32, kind="ExternalOutput").ap())
    build(nc, *args)
    r = _run(nc, [arrays], core_ids=[0])
    return r.results[0]["out_0"]
```
